# Optimizing a Trainium2 kernel written in Bass

```python
import numpy as np
import jax
import jax.numpy as jnp

def _softmax(x, axis=-1):
    return jax.nn.softmax(x, axis=axis)

def _gelu(x):
    return jax.nn.gelu(x, approximate=True)

def _silu(x):
    return jax.nn.silu(x)

def _sigmoid(x):
    return jax.nn.sigmoid(x)

def _layernorm(x, axis=-1, eps=1e-05):
    m = jnp.mean(x, axis=axis, keepdims=True)
    v = jnp.var(x, axis=axis, keepdims=True)
    return (x - m) / jnp.sqrt(v + eps)

def _scatter_add(tgt, idx, src, axis=0):
    return tgt.at[idx].add(src)

def _segment_sum(src, seg, n):
    return jax.ops.segment_sum(src, seg, n)
kernel_name = 'mk_adaln_d2_jaxref_r8_4a6d74'

def setup_inputs(seed: int=0):
    np.random.seed(seed)
    _w = jnp.asarray

    def _L0_attn_setup():
        import jax, jax.numpy as jnp
        import numpy as np
        D_MODEL, N_HEADS, N_KV, HEAD_DIM, D_LAT = (128, 8, 2, 128, 32)
        N_REP = N_HEADS // N_KV
        B, T = (2, 256)
        key = jax.random.key(seed)
        ks = jax.random.split(key, 8)
        s = lambda fan_in: 1.0 / np.sqrt(fan_in)
        return {'x': jax.random.normal(ks[0], (B, T, D_MODEL), jnp.float32), 'wq': jax.random.normal(ks[1], (D_MODEL, N_HEADS * HEAD_DIM), jnp.float32) * s(D_MODEL), 'wk_down': jax.random.normal(ks[2], (D_MODEL, N_KV * D_LAT), jnp.float32) * s(D_MODEL), 'wv_down': jax.random.normal(ks[3], (D_MODEL, N_KV * D_LAT), jnp.float32) * s(D_MODEL), 'wk_up': jax.random.normal(ks[4], (D_LAT, HEAD_DIM), jnp.float32) * s(D_LAT), 'wv_up': jax.random.normal(ks[5], (D_LAT, HEAD_DIM), jnp.float32) * s(D_LAT), 'wo': jax.random.normal(ks[6], (N_HEADS * HEAD_DIM, D_MODEL), jnp.float32) * s(N_HEADS * HEAD_DIM)}
    _L0_attn_in = _L0_attn_setup()

    def _L0_ffn_setup():
        import jax, jax.numpy as jnp
        import numpy as np
        E = 8
        TOP_K = 2
        H = 128
        I = 64
        B, S = (2, 256)

        def _moe_forward(hidden_states, w_gate, w_fc, w_proj):
            b, s, h = hidden_states.shape
            x = hidden_states.reshape(-1, h)
            T = x.shape[0]
            router_logits = x @ w_gate.T
            topk_vals, topk_idx = jax.lax.top_k(router_logits, TOP_K)
            router_weights = jax.nn.softmax(topk_vals.astype(jnp.float32), axis=-1).astype(x.dtype)
            gates = jnp.zeros((T, E), x.dtype).at[jnp.arange(T)[:, None], topk_idx].add(router_weights)
            hmid = jax.nn.gelu(jnp.einsum('th,eih->tei', x, w_fc), approximate=False)
            y = jnp.einsum('tei,ehi->teh', hmid, w_proj)
            out = jnp.einsum('teh,te->th', y, gates)
            return out.reshape(b, s, h)
        key = jax.random.key(seed)
        k0, k1, k2, k3 = jax.random.split(key, 4)
        std = 0.02
        return {'hidden_states': jax.random.normal(k0, (B, S, H), dtype=jnp.float32), 'w_gate': jax.random.normal(k1, (E, H), dtype=jnp.float32) * std, 'w_fc': jax.random.normal(k2, (E, I, H), dtype=jnp.float32) * std, 'w_proj': jax.random.normal(k3, (E, H, I), dtype=jnp.float32) * (std / np.sqrt(48.0))}
    _L0_ffn_in = _L0_ffn_setup()
    _L0_c = _w((lambda *s: np.random.randn(*s).astype(np.float32) * 0.05)(8, 128))
    _L0_wmod = _w((lambda *s: np.random.randn(*s).astype(np.float32) * 0.05)(128, 6 * 128) * 128 ** (-0.5))

    def _L1_attn_setup():
        import jax, jax.numpy as jnp
        import numpy as np
        D_MODEL = 128
        D_STATE = 16
        D_CONV = 4
        EXPAND = 2
        D_INNER = EXPAND * D_MODEL
        BATCH = 2
        SEQ = 128
        key = jax.random.key(seed)
        ks = jax.random.split(key, 12)
        s = 0.02
        return {'x': jax.random.normal(ks[0], (BATCH, SEQ, D_MODEL), jnp.float32), 'in_proj_w': jax.random.normal(ks[1], (D_MODEL, 2 * D_INNER), jnp.float32) * s, 'in_proj_b': jnp.zeros((2 * D_INNER,), jnp.float32), 'conv_w': jax.random.normal(ks[2], (D_CONV, D_INNER), jnp.float32) * s, 'conv_b': jnp.zeros((D_INNER,), jnp.float32), 'x_proj_w': jax.random.normal(ks[3], (D_INNER, 3 * D_STATE), jnp.float32) * s, 'x_proj_b': jnp.zeros((3 * D_STATE,), jnp.float32), 'dt_proj_w': jax.random.normal(ks[4], (D_STATE, D_INNER), jnp.float32) * s, 'dt_proj_b': jnp.full((D_INNER,), -2.0, jnp.float32), 'A_log': jnp.tile(jnp.log(jnp.arange(1, D_STATE + 1, dtype=jnp.float32)), (D_INNER, 1)), 'D_skip': jnp.ones((D_INNER,), jnp.float32), 'out_proj_w': jax.random.normal(ks[5], (D_INNER, D_MODEL), jnp.float32) * s, 'out_proj_b': jnp.zeros((D_MODEL,), jnp.float32)}
    _L1_attn_in = _L1_attn_setup()

    def _L1_ffn_setup():
        import jax, jax.numpy as jnp
        import numpy as np
        B, S, D, E, F, TOP_K = (4, 256, 128, 8, 512, 2)
        key = jax.random.key(seed)
        k0, k1, k2, k3 = jax.random.split(key, 4)
        init = lambda k, shape, fan: (jax.random.normal(k, shape, jnp.float32) / np.sqrt(fan)).astype(jnp.float32)
        return {'x': jax.random.normal(k0, (B, S, D), jnp.float32), 'gate_w': init(k1, (D, E), D), 'w1': init(k2, (E, D, F), D), 'b1': jnp.zeros((E, F), jnp.float32), 'w2': init(k3, (E, F, D), F), 'b2': jnp.zeros((E, D), jnp.float32)}
    _L1_ffn_in = _L1_ffn_setup()
    _L1_c = _w((lambda *s: np.random.randn(*s).astype(np.float32) * 0.05)(8, 128))
    _L1_wmod = _w((lambda *s: np.random.randn(*s).astype(np.float32) * 0.05)(128, 6 * 128) * 128 ** (-0.5))
    _d = {'L0_attn_x': _L0_attn_in['x'], 'L0_attn_wq': _L0_attn_in['wq'], 'L0_attn_wk_down': _L0_attn_in['wk_down'], 'L0_attn_wv_down': _L0_attn_in['wv_down'], 'L0_attn_wk_up': _L0_attn_in['wk_up'], 'L0_attn_wv_up': _L0_attn_in['wv_up'], 'L0_attn_wo': _L0_attn_in['wo'], 'L0_ffn_w_gate': _L0_ffn_in['w_gate'], 'L0_ffn_w_fc': _L0_ffn_in['w_fc'], 'L0_ffn_w_proj': _L0_ffn_in['w_proj'], 'L0_c': _L0_c, 'L0_wmod': _L0_wmod, 'L1_attn_in_proj_w': _L1_attn_in['in_proj_w'], 'L1_attn_in_proj_b': _L1_attn_in['in_proj_b'], 'L1_attn_conv_w': _L1_attn_in['conv_w'], 'L1_attn_conv_b': _L1_attn_in['conv_b'], 'L1_attn_x_proj_w': _L1_attn_in['x_proj_w'], 'L1_attn_x_proj_b': _L1_attn_in['x_proj_b'], 'L1_attn_dt_proj_w': _L1_attn_in['dt_proj_w'], 'L1_attn_dt_proj_b': _L1_attn_in['dt_proj_b'], 'L1_attn_A_log': _L1_attn_in['A_log'], 'L1_attn_D_skip': _L1_attn_in['D_skip'], 'L1_attn_out_proj_w': _L1_attn_in['out_proj_w'], 'L1_attn_out_proj_b': _L1_attn_in['out_proj_b'], 'L1_ffn_gate_w': _L1_ffn_in['gate_w'], 'L1_ffn_w1': _L1_ffn_in['w1'], 'L1_ffn_b1': _L1_ffn_in['b1'], 'L1_ffn_w2': _L1_ffn_in['w2'], 'L1_ffn_b2': _L1_ffn_in['b2'], 'L1_c': _L1_c, 'L1_wmod': _L1_wmod}
    _x0 = _d['L0_attn_x']
    _d['L0_attn_x'] = jax.random.normal(jax.random.fold_in(jax.random.key(seed), 1), (8, 512, 128), dtype=_x0.dtype)
    del _x0
    return _d

def reference(L0_attn_x, L0_attn_wq, L0_attn_wk_down, L0_attn_wv_down, L0_attn_wk_up, L0_attn_wv_up, L0_attn_wo, L0_ffn_w_gate, L0_ffn_w_fc, L0_ffn_w_proj, L0_c, L0_wmod, L1_attn_in_proj_w, L1_attn_in_proj_b, L1_attn_conv_w, L1_attn_conv_b, L1_attn_x_proj_w, L1_attn_x_proj_b, L1_attn_dt_proj_w, L1_attn_dt_proj_b, L1_attn_A_log, L1_attn_D_skip, L1_attn_out_proj_w, L1_attn_out_proj_b, L1_ffn_gate_w, L1_ffn_w1, L1_ffn_b1, L1_ffn_w2, L1_ffn_b2, L1_c, L1_wmod):

    def _L0_attn_ref(x, wq, wk_down, wv_down, wk_up, wv_up, wo):
        import jax, jax.numpy as jnp
        import numpy as np
        D_MODEL, N_HEADS, N_KV, HEAD_DIM, D_LAT = (128, 8, 2, 128, 32)
        N_REP = N_HEADS // N_KV
        B, T = (2, 256)
        Bq, Tq, _ = x.shape
        scale = HEAD_DIM ** (-0.5)
        q = (x @ wq).reshape(Bq, Tq, N_KV, N_REP, HEAD_DIM)
        k_lat = (x @ wk_down).reshape(Bq, Tq, N_KV, D_LAT)
        v_lat = (x @ wv_down).reshape(Bq, Tq, N_KV, D_LAT)
        k = jnp.einsum('bkhl,ld->bkhd', k_lat, wk_up)
        v = jnp.einsum('bkhl,ld->bkhd', v_lat, wv_up)
        scores = jnp.einsum('bqhrd,bkhd->bhrqk', q, k) * scale
        causal = jnp.tril(jnp.ones((Tq, Tq), dtype=bool))
        scores = jnp.where(causal, scores, jnp.finfo(scores.dtype).min)
        probs = jax.nn.softmax(scores, axis=-1)
        y = jnp.einsum('bhrqk,bkhd->bqhrd', probs, v)
        y = y.reshape(Bq, Tq, N_HEADS * HEAD_DIM)
        return y @ wo

    def _L0_ffn_ref(hidden_states, w_gate, w_fc, w_proj):
        import jax, jax.numpy as jnp
        import numpy as np
        E = 8
        TOP_K = 2
        H = 128
        I = 64
        B, S = (2, 256)

        def _moe_forward(hidden_states, w_gate, w_fc, w_proj):
            b, s, h = hidden_states.shape
            x = hidden_states.reshape(-1, h)
            T = x.shape[0]
            router_logits = x @ w_gate.T
            topk_vals, topk_idx = jax.lax.top_k(router_logits, TOP_K)
            router_weights = jax.nn.softmax(topk_vals.astype(jnp.float32), axis=-1).astype(x.dtype)
            gates = jnp.zeros((T, E), x.dtype).at[jnp.arange(T)[:, None], topk_idx].add(router_weights)
            hmid = jax.nn.gelu(jnp.einsum('th,eih->tei', x, w_fc), approximate=False)
            y = jnp.einsum('tei,ehi->teh', hmid, w_proj)
            out = jnp.einsum('teh,te->th', y, gates)
            return out.reshape(b, s, h)
        return _moe_forward(hidden_states, w_gate, w_proj=w_proj, w_fc=w_fc)

    def _L1_attn_ref(x, in_proj_w, in_proj_b, conv_w, conv_b, x_proj_w, x_proj_b, dt_proj_w, dt_proj_b, A_log, D_skip, out_proj_w, out_proj_b):
        import jax, jax.numpy as jnp
        import numpy as np
        D_MODEL = 128
        D_STATE = 16
        D_CONV = 4
        EXPAND = 2
        D_INNER = EXPAND * D_MODEL
        BATCH = 2
        SEQ = 128
        b, l, _ = x.shape
        xr = x @ in_proj_w + in_proj_b
        x_in, res = (xr[..., :D_INNER], xr[..., D_INNER:])
        xp = jnp.pad(x_in, ((0, 0), (D_CONV - 1, 0), (0, 0)))
        xc = conv_b + sum((xp[:, k:k + l, :] * conv_w[k] for k in range(D_CONV)))
        xc = jax.nn.silu(xc)
        proj = xc @ x_proj_w + x_proj_b
        d_raw, Bm, Cm = jnp.split(proj, 3, axis=-1)
        delta = jax.nn.softplus(d_raw @ dt_proj_w + dt_proj_b)
        A = -jnp.exp(A_log)
        dA = jnp.exp(delta[..., None] * A)
        dBx = (delta * xc)[..., None] * Bm[:, :, None, :]

        def step(h, inp):
            dA_t, dBx_t, c_t = inp
            h = dA_t * h + dBx_t
            y = jnp.einsum('bdn,bn->bd', h, c_t)
            return (h, y)
        h0 = jnp.zeros((b, D_INNER, D_STATE), xc.dtype)
        xs = (dA.transpose(1, 0, 2, 3), dBx.transpose(1, 0, 2, 3), Cm.transpose(1, 0, 2))
        _, ys = jax.lax.scan(step, h0, xs)
        y = ys.transpose(1, 0, 2) + xc * D_skip
        return y * jax.nn.silu(res) @ out_proj_w + out_proj_b

    def _L1_ffn_ref(x, gate_w, w1, b1, w2, b2):
        import jax, jax.numpy as jnp
        import numpy as np
        B, S, D, E, F, TOP_K = (4, 256, 128, 8, 512, 2)
        b, s, d = x.shape
        e = gate_w.shape[1]
        xf = x.reshape(-1, d)
        t = xf.shape[0]
        logits = xf @ gate_w
        top_w, top_idx = jax.lax.top_k(logits, TOP_K)
        top_w = jax.nn.softmax(top_w.astype(jnp.float32), axis=-1).astype(x.dtype)
        combine = jnp.zeros((t, e), x.dtype).at[jnp.arange(t)[:, None], top_idx].add(top_w)
        h = jax.nn.gelu(jnp.einsum('td,edf->tef', xf, w1) + b1, approximate=False)
        y = jnp.einsum('tef,efd->ted', h, w2) + b2
        out = jnp.einsum('ted,te->td', y, combine)
        return out.reshape(b, s, d)
    x = L0_attn_x
    mod = (_silu(L0_c) @ L0_wmod).reshape(L0_c.shape[0], 6, 1, -1)
    sa, ca, ga, sb, cb, gb = (mod[:, 0], mod[:, 1], mod[:, 2], mod[:, 3], mod[:, 4], mod[:, 5])
    ga = (2 * (ga >= 0) - 1) * jnp.maximum(jnp.abs(ga), 0.25)
    gb = (2 * (gb >= 0) - 1) * jnp.maximum(jnp.abs(gb), 0.25)
    h = _layernorm(x, axis=-1) * (1 + ca) + sa
    x = x + ga * _L0_attn_ref(h, L0_attn_wq, L0_attn_wk_down, L0_attn_wv_down, L0_attn_wk_up, L0_attn_wv_up, L0_attn_wo)
    h = _layernorm(x, axis=-1) * (1 + cb) + sb
    x = x + gb * _L0_ffn_ref(h, L0_ffn_w_gate, L0_ffn_w_fc, L0_ffn_w_proj)
    mod = (_silu(L1_c) @ L1_wmod).reshape(L1_c.shape[0], 6, 1, -1)
    sa, ca, ga, sb, cb, gb = (mod[:, 0], mod[:, 1], mod[:, 2], mod[:, 3], mod[:, 4], mod[:, 5])
    ga = (2 * (ga >= 0) - 1) * jnp.maximum(jnp.abs(ga), 0.25)
    gb = (2 * (gb >= 0) - 1) * jnp.maximum(jnp.abs(gb), 0.25)
    h = _layernorm(x, axis=-1) * (1 + ca) + sa
    x = x + ga * _L1_attn_ref(h, L1_attn_in_proj_w, L1_attn_in_proj_b, L1_attn_conv_w, L1_attn_conv_b, L1_attn_x_proj_w, L1_attn_x_proj_b, L1_attn_dt_proj_w, L1_attn_dt_proj_b, L1_attn_A_log, L1_attn_D_skip, L1_attn_out_proj_w, L1_attn_out_proj_b)
    h = _layernorm(x, axis=-1) * (1 + cb) + sb
    x = x + gb * _L1_ffn_ref(h, L1_ffn_gate_w, L1_ffn_w1, L1_ffn_b1, L1_ffn_w2, L1_ffn_b2)
    return x

_drawn_inputs = setup_inputs


def setup_inputs(seed=0):
    import zlib

    import numpy as np

    out = dict(_drawn_inputs(seed))
    spreads = {'L1_attn_in_proj_b': (0.0, 0.8),
     'L1_attn_conv_b': (0.0, 0.8),
     'L1_attn_x_proj_b': (0.0, 0.8),
     'L1_attn_dt_proj_b': (-2.0, 0.6),
     'L1_attn_D_skip': (1.0, 0.6),
     'L1_attn_out_proj_b': (0.0, 0.782),
     'L1_ffn_b1': (0.0, 1.81),
     'L1_ffn_b2': (0.0, 1.218)}
    factors = {'L0_ffn_w_gate': 8.0,
     'L0_ffn_w_fc': 8.0,
     'L0_ffn_w_proj': 8.0,
     'L1_attn_in_proj_w': 8.0,
     'L1_attn_conv_w': 8.0,
     'L1_attn_x_proj_w': 8.0,
     'L1_attn_dt_proj_w': 8.0,
     'L1_attn_A_log': 8.0,
     'L1_attn_out_proj_w': 8.0}
    for name, (base, spread) in spreads.items():
        noise = np.random.default_rng([zlib.crc32(name.encode()), seed]).standard_normal(out[name].shape)
        drawn = base * np.exp(spread * noise) if base else spread * noise
        out[name] = jnp.asarray(drawn.astype(out[name].dtype))
    for name, factor in factors.items():
        out[name] = (out[name] * factor).astype(out[name].dtype)
    return out
```

```python
from contextlib import ExitStack

import numpy as np

import concourse.bass as bass
from concourse import mybir

F32 = mybir.dt.float32
BF16 = mybir.dt.bfloat16
ALU = mybir.AluOpType
ACT = mybir.ActivationFunctionType
AX_X = mybir.AxisListType.X

P = 128
B = 8
T = 512
NT = T // P
H = 8
G = 2
HG = H // G
L = 32
E = 8
F0 = 64
C0 = E * F0 // P
F1 = 512
C1 = F1 // P
DI = 256
DH = DI // P
NS = 16
KC = 4
BC = 2 * NS
PR = 3 * BC + NS
EPS = 1e-5
SCALE = float(P) ** -0.5
FAR = -3.0e38


class Signal:

    def __init__(self, sem, per_batch, primed):
        self.sem, self.per_batch, self.primed = sem, per_batch, primed

    def at(self, b, n):
        return b * self.per_batch + n + self.primed

    def before(self, b):
        assert self.primed
        return b * self.per_batch + self.primed


def build(nc, io, out):
    ctx = ExitStack()
    with ctx:
        def sb(name, shape, dt=F32):
            return ctx.enter_context(nc.sbuf_tensor(name, shape, dt))

        def sem(name):
            return ctx.enter_context(nc.semaphore(name))

        def signal(name, per_batch, primed=0):
            return Signal(sem(name), per_batch, primed)

        probs_T = sb("probs_T", [P, HG, NT, T])
        setup_space = probs_T[:].rearrange("p h k q -> p (h k q)")
        setup_only = {"wqT": 0, "wo": H * P, "wmod": 2 * H * P}
        w = {name: sb("w_" + name, list(ap.shape)) for name, ap in io.items() if name not in ("x", *setup_only)}
        w["wqT"] = setup_space[:, 0:H * P].rearrange("p (h d) -> p h d", h=H)
        w["wo"] = setup_space[:, H * P:2 * H * P].rearrange("p (h d) -> p h d", h=H)
        w["wmod"] = setup_space[:, 2 * H * P:2 * H * P + 12 * P].rearrange("p (l d) -> p l d", l=2)
        silu_wide = setup_space[:, 4 * H * P:4 * H * P + 2 * B * P].rearrange("p (l b d) -> p l b d", l=2, b=B)
        ident = w["ident"]

        ident_bf = sb("ident_bf", [P, P], BF16)
        mask_bf = sb("mask_bf", [P, P], BF16)
        select = sb("select", [3 * BC, BC, P], BF16)
        silu_c = sb("silu_c", [P, 2, B])
        silu_half = sb("silu_half", [P, 2, B])
        silu_tanh = sb("silu_tanh", [P, 2, B])
        mod = sb("mod", [P, 2, 6, B])
        gate = sb("gate", [P, B, 4, P])
        gate_sign = sb("gate_sign", [P, 4, P])
        gate_size = sb("gate_size", [P, 4, P])
        gate_two = sb("gate_two", [P, 4, P])
        w_qk = sb("w_qk", [P, G, HG * L])
        w_vo = sb("w_vo", [P, G, P])
        a_neg = sb("a_neg", [P, DH, NS])
        a_exp = sb("a_exp", [P, DH, NS])
        eps_col = sb("eps_col", [P, 1])

        x_in = sb("x_in", [P, NT, P])
        x = sb("x", [P, NT, P])
        x_out = sb("x_out", [P, NT, P])
        mixed = sb("mixed", [P, NT, P])
        stats = sb("stats", [P, NT, 6])
        meanvar = sb("meanvar", [P, NT, 2])
        log_var = sb("log_var", [P, NT])
        rstd0 = sb("rstd0", [P, NT])
        var_eps = sb("var_eps", [P, NT])
        newton = sb("newton", [P, NT])
        newton2 = sb("newton2", [P, NT])
        newton3 = sb("newton3", [P, NT])
        rstd = sb("rstd", [P, NT])
        shift = sb("shift", [P, NT])
        xn = sb("xn", [P, NT, P])
        hT = [sb(f"hT{j}", [P, T]) for j in range(4)]

        hidden = sb("hidden", [P, 2 * C1, T])
        q_lat = hidden[:, 0:G, :]
        k_pad = sb("k_pad", [P, G, HG, T])
        v_lat = hidden[:, 6, 0:NT * G * L].rearrange("p (t m) -> p t m", t=NT)
        row_neg = sb("row_neg", [P, 2, 2])
        row_max = sb("row_max", [P, 2, 2])
        probs = sb("probs", [P, 2, 2, T])
        row_sum = sb("row_sum", [P, G, NT, HG])
        row_inv = sb("row_inv", [P, NT, HG])
        inv_wide = hidden[:, 4, :].rearrange("p (t h l) -> p t h l", t=NT, h=HG)
        inv_T = hidden[:, 5, :]
        y_T = hidden[:, G:2 * G, :]

        logits = sb("logits", [P, NT, E])
        r_a = sb("r_a", [P, NT, E])
        r_b = sb("r_b", [P, NT, E])
        top = sb("top", [P, 2, NT])
        best = sb("best", [P, 2, NT])
        pick1 = sb("pick1", [P, NT, E])
        pick2 = sb("pick2", [P, NT, E])
        gap = sb("gap", [P, NT])
        gap_exp = sb("gap_exp", [P, NT])
        gap_one = sb("gap_one", [P, NT])
        share1 = sb("share1", [P, NT])
        share2 = sb("share2", [P, NT])
        gates = sb("gates", [P, NT, E])
        gates_wide = probs[:].rearrange("p a b (c f) -> p (a b) c f", f=F0)
        gates_T = sb("gates_T", [E, T])

        gated = hidden[:, C1:2 * C1, :]
        expert_sum = sb("expert_sum", [P, NT, P])

        xi = sb("xi", [P, DH, T + KC - 1])
        mix_space = probs_T[:].rearrange("p h k q -> p (h k q)")

        def within(first, *shape):
            n = int(np.prod(shape))
            flat = mix_space[:, first * T:(first + n) * T]
            if len(shape) == 1:
                return flat.rearrange("p (a t) -> p a t", a=shape[0])
            return flat.rearrange("p (a c t) -> p a c t", a=shape[0], c=shape[1])

        decay = within(0, 4, DH)
        inject = within(8, 2, DH)
        state = within(12, 2, DH)
        read = probs
        conv = [within(0, DH), within(DH, DH)]
        tanh_c = within(8, DH)
        res = within(12, DH)
        part = mix_space[0:3 * BC, 14 * T:15 * T]
        part2 = mix_space[0:3 * BC, 15 * T:16 * T]
        dt_exp, dt_abs, dt_log, z = conv[0], conv[1], tanh_c, conv[0]
        xc = sb("xc", [P, DH, T])
        res_gate = sb("res_gate", [P, DH, T])
        proj = sb("proj", [PR, T])
        split = sb("split", [3 * BC, T], BF16)
        dt_in = sb("dt_in", [P, DH, T])
        y_skip = dt_in
        delta = sb("delta", [P, DH, T])
        u = sb("u", [P, DH, T])

        bank = [ctx.enter_context(nc.psum_tensor(f"bank{i}", [P, T], F32)) for i in range(8)]
        score = [ctx.enter_context(nc.psum_tensor(f"score{i}", [P, 2, T], F32)) for i in range(0)]
        BC_BANK, Y_BANK, HID_BANK, OUT_BANK, MISC = (0, 1), (2, 3), (4, 5), 6, 7

        weights_in = sem("weights_in")
        setup_v, setup_a, setup_p, setup_v2 = sem("setup_v"), sem("setup_a"), sem("setup_p"), sem("setup_v2")
        x_loaded = signal("x_loaded", 16)
        x_stored = signal("x_stored", 16)
        x_sent = signal("x_sent", 1, primed=1)
        x_taken = signal("x_taken", 1, primed=1)
        x_final = signal("x_final", 1)
        chain = signal("chain", CHAIN_PER_BATCH)
        chain_a = signal("chain_a", CHAIN_A_PER_BATCH)
        ln_var = signal("ln_var", 4)
        ln_r0 = signal("ln_r0", 4)
        ln_xn = signal("ln_xn", 4)
        ln_T = signal("ln_T", 4)
        h_ready = signal("h_ready", 4)

        q_mm = signal("q_mm", 2 * G)
        q_out = signal("q_out", G)
        k_out = signal("k_out", G)
        v_mm = signal("v_mm", 1)
        v_out = signal("v_out", 1)
        UNITS = G * NT * 2
        s_mm = signal("s_mm", UNITS)
        s_max = signal("s_max", UNITS)
        s_exp = signal("s_exp", UNITS)
        p_T = signal("p_T", 2 * UNITS)
        p_out = signal("p_out", 2 * UNITS)
        y_mm = signal("y_mm", G)
        inv_w = signal("inv_w", G)
        inv_mm = signal("inv_mm", G)
        inv_out = signal("inv_out", G)
        y_out = signal("y_out", G)
        attn_mm = signal("attn_mm", 1)
        attn_add = signal("attn_add", 1)

        log_mm = signal("log_mm", 2)
        gap_in = signal("gap_in", 2)
        gap_out = signal("gap_out", 2)
        gates_ok = signal("gates_ok", 2, primed=1)
        hid0_mm = signal("hid0_mm", C0)
        hid0_act = signal("hid0_act", C0)
        gT_mm = signal("gT_mm", C0)
        hid0_gate = signal("hid0_gate", C0)
        out0_mm = signal("out0_mm", 1)
        out0_add = signal("out0_add", 1)

        in_mm = signal("in_mm", 2 * DH)
        in_out = signal("in_out", 2 * DH)
        conv_ok = signal("conv_ok", DH)
        tanh_ok = signal("tanh_ok", 2 * DH)
        xc_ok = signal("xc_ok", DH)
        pr_mm = signal("pr_mm", 1)
        pr_out = signal("pr_out", 1)
        split_ok = signal("split_ok", 1)
        dt_mm = signal("dt_mm", DH)
        dt_z = signal("dt_z", DH)
        dt_l = signal("dt_l", DH)
        delta_ok = signal("delta_ok", DH)
        u_ok = signal("u_ok", DH)
        dec_ok = signal("dec_ok", NS * DH)
        b_mm = signal("b_mm", NS)
        c_mm = signal("c_mm", NS)
        inj_ok = signal("inj_ok", NS * DH)
        st_ok = signal("st_ok", NS * DH)
        rd_ok = signal("rd_ok", NS * DH)
        sum_mm = signal("sum_mm", NS * DH)
        z_ok = signal("z_ok", DH, primed=1)
        mix_mm = signal("mix_mm", 1)
        mix_add = signal("mix_add", 1)

        gt_mm = signal("gt_mm", 1)
        gt_out = signal("gt_out", 1)
        b2_mm = signal("b2_mm", 1)
        hid1_mm = signal("hid1_mm", E * C1, primed=1)
        hid1_act = signal("hid1_act", E * C1)
        out1_mm = signal("out1_mm", E, primed=1)
        out1_add = signal("out1_add", E + 1, primed=1)

        n_weights = len(w)
        block = ctx.enter_context(nc.Block())

        @block.sync
        def _(sp):
            for name, tile in w.items():
                sp.dma_start(tile[:], io[name]).then_inc(weights_in, 16)
            for s in (gates_ok, hid1_mm, out1_add, out1_mm, x_sent, x_taken, z_ok):
                sp.sem_inc(s.sem, 1)

        @block.gpsimd
        def _(pool):
            x_rows = io["x"].rearrange("b (t p) d -> b p t d", p=P)
            out_rows = out.rearrange("b (t p) d -> b p t d", p=P)
            with pool.Fori(0, B) as b:
                pool.wait_ge(x_taken.sem, x_taken.before(b))
                pool.dma_start(x_in[:], x_rows[bass.ds(b, 1), :, :, :].rearrange("a p t d -> p (a t) d")
                             ).then_inc(x_loaded.sem, 16)
                pool.wait_ge(x_final.sem, x_final.at(b, 1))
                pool.dma_start(out_rows[bass.ds(b, 1), :, :, :].rearrange("a p t d -> p (a t) d"), x_out[:]
                             ).then_inc(x_stored.sem, 16)
                pool.wait_ge(x_stored.sem, x_stored.at(b, 16))
                pool.sem_inc(x_sent.sem, 1)

        @block.tensor
        def _(pe):
            mm, tr = nc.tensor.matmul, nc.tensor.transpose

            pe.wait_ge(weights_in, 16 * n_weights)
            for h in range(H):
                ins = mm(bank[0][:, h * L:(h + 1) * L], w["wqT"][:, h, :], w["wk_upT"][:], start=True, stop=True)
            for h in range(H):
                g, j = divmod(h, HG)
                ins = mm(bank[1][j * L:(j + 1) * L, g * P:(g + 1) * P], w["wv_upT"][:], w["wo"][:, h, :],
                         start=True, stop=True)
            pe.wait_ge(setup_v, 3)
            for l in range(2):
                for j in range(6):
                    ins = mm(bank[2][:, (l * 6 + j) * B:(l * 6 + j + 1) * B], w["wmod"][:, l, j * P:(j + 1) * P],
                             silu_c[:, l, :], start=True, stop=True)
            ins.then_inc(setup_p, 1)
            for b in range(B):
                if b >= 2:
                    pe.wait_ge(setup_v, 7 + b - 1)
                for k in range(4):
                    l, j = k // 2, 2 if k % 2 == 0 else 5
                    ins = mm(bank[3 + b % 2][:, k * P:(k + 1) * P], silu_wide[:, l, b, :],
                             w["wmod"][:, l, j * P:(j + 1) * P], start=True, stop=True)
                ins.then_inc(setup_p, 1)
            pe.wait_ge(setup_v, SETUP_V)
            pe.wait_ge(setup_a, SETUP_A)

            def layernorm(b, j, free, value):
                pe.wait_ge(ln_xn.sem, ln_xn.at(b, j + 1))
                pe.wait_ge(free.sem, value)
                for t in range(NT):
                    ins = tr(bank[MISC][:, t * P:(t + 1) * P], xn[:, t, :], ident[:])
                ins.then_inc(ln_T.sem, 1)
                pe.wait_ge(h_ready.sem, h_ready.at(b, j + 1))

            def router(b, layer, weight):
                for t in range(NT):
                    ins = mm(bank[MISC][:, t * E:(t + 1) * E], hT[2 * layer + 1][:, t * P:(t + 1) * P], weight[:],
                             start=True, stop=True)
                ins.then_inc(log_mm.sem, 1)

            with pe.Fori(0, B) as b:
                layernorm(b, 0, gates_ok, gates_ok.before(b))
                pe.wait_ge(out1_add.sem, out1_add.before(b))
                for g in range(G):
                    pe_bank = bank[4 + g]
                    mm(pe_bank[:], w_qk[:, g, :], hT[0][:], start=True, stop=True).then_inc(q_mm.sem, 1)
                pe.wait_ge(z_ok.sem, z_ok.before(b))
                for g in range(G):
                    mm(bank[2 + g][:], w["wk4"][:, g, :], hT[0][:], start=True, stop=True).then_inc(q_mm.sem, 1)
                for t in range(NT):
                    ins = mm(bank[OUT_BANK][:, t * G * L:(t + 1) * G * L], hT[0][:, t * P:(t + 1) * P], w["wv_down"][:],
                             start=True, stop=True)
                ins.then_inc(v_mm.sem, 1)

                def scores(n):
                    g, i, pair = n // (2 * NT), n // 2 % NT, n % 2
                    if i == 0 and pair == 0:
                        pe.wait_ge(q_out.sem, q_out.at(b, g + 1))
                        pe.wait_ge(k_out.sem, k_out.at(b, g + 1))
                    if n == 1:
                        pe.wait_ge(k_out.sem, k_out.at(b, G))
                    if n >= 2:
                        pe.wait_ge(s_exp.sem, s_exp.at(b, n - 1))
                    for jj in range(2):
                        j = 2 * pair + jj
                        s = bank[2 * (n % 2) + jj]
                        mm(s[:, 0:(i + 1) * P], q_lat[:, g, i * P:(i + 1) * P], k_pad[:, g, j, 0:(i + 1) * P],
                           start=True, stop=False)
                        ins = mm(s[:, i * P:(i + 1) * P], ident_bf[:], mask_bf[:], start=False, stop=True)
                    ins.then_inc(s_mm.sem, 1)

                def transposes(n):
                    i = n // 2 % NT
                    pe.wait_ge(s_exp.sem, s_exp.at(b, n + 1))
                    for jj in range(2):
                        if n == 0:
                            pe.wait_ge(q_out.sem, q_out.at(b, G))
                        else:
                            pe.wait_ge(p_out.sem, p_out.at(b, 2 * n + jj - 1))
                        for k in range(i + 1):
                            ins = tr(bank[4 + jj][:, k * P:(k + 1) * P], probs[:, n % 2, jj, k * P:(k + 1) * P], ident[:])
                        ins.then_inc(p_T.sem, 1)

                def values(g):
                    pe.wait_ge(p_out.sem, p_out.at(b, (g + 1) * 4 * NT))
                    pe.wait_ge(v_out.sem, v_out.at(b, 1))
                    if g > 0:
                        pe.wait_ge(y_out.sem, y_out.at(b, g))
                    for k in range(NT):
                        for j in range(HG):
                            ins = mm(bank[OUT_BANK][j * L:(j + 1) * L, k * P:T], v_lat[:, k, g * L:(g + 1) * L],
                                     probs_T[:, j, k, k * P:T], start=(k == 0), stop=(k == NT - 1),
                                     skip_group_check=True)
                    ins.then_inc(y_mm.sem, 1)
                    pe.wait_ge(inv_w.sem, inv_w.at(b, g + 1))
                    for t in range(NT):
                        ins = tr(bank[MISC][:, t * P:(t + 1) * P], inv_wide[:, t, :, :].rearrange("p h l -> p (h l)"),
                                 ident[:])
                    ins.then_inc(inv_mm.sem, 1)

                for n in range(UNITS + 1):
                    if n < UNITS:
                        scores(n)
                    if n >= 1:
                        transposes(n - 1)
                    if n == UNITS // 2 + 1:
                        values(0)
                values(1)
                pe.wait_ge(y_out.sem, y_out.at(b, G))
                for t in range(NT):
                    for g in range(G):
                        ins = mm(bank[MISC][:, t * P:(t + 1) * P], y_T[:, g, t * P:(t + 1) * P], w_vo[:, g, :],
                                 start=(g == 0), stop=(g == G - 1))
                ins.then_inc(attn_mm.sem, 1)

                layernorm(b, 1, attn_add, attn_add.at(b, 1))
                router(b, 0, w["wg0"])
                for c in range(C0):
                    if c >= 2:
                        pe.wait_ge(hid0_act.sem, hid0_act.at(b, c - 1))
                    mm(bank[HID_BANK[c % 2]][:], w["wfcT"][:, c * P:(c + 1) * P], hT[1][:], start=True, stop=True
                       ).then_inc(hid0_mm.sem, 1)
                pe.wait_ge(gates_ok.sem, gates_ok.at(b, 1))
                for c in range(C0):
                    if c >= 2:
                        pe.wait_ge(hid0_gate.sem, hid0_gate.at(b, c - 1))
                    for t in range(NT):
                        wide = gates_wide[:, t, :, :].rearrange("p e f -> p (e f)")
                        ins = tr(bank[c % 2][:, t * P:(t + 1) * P], wide[:, c * P:(c + 1) * P], ident[:])
                    ins.then_inc(gT_mm.sem, 1)
                pe.wait_ge(hid0_gate.sem, hid0_gate.at(b, C0))
                for t in range(NT):
                    for c in range(C0):
                        ins = mm(bank[OUT_BANK][:, t * P:(t + 1) * P], gated[:, c, t * P:(t + 1) * P],
                                 w["wprojT"][:, c, :], start=(c == 0), stop=(c == C0 - 1))
                ins.then_inc(out0_mm.sem, 1)

                layernorm(b, 2, gates_ok, gates_ok.at(b, 1))
                for c in range(2 * DH):
                    if c >= 2:
                        pe.wait_ge(in_out.sem, in_out.at(b, c - 1))
                    mm(bank[HID_BANK[c % 2]][:], w["in_w"][:, c * P:(c + 1) * P], hT[2][:], start=True, stop=True
                       ).then_inc(in_mm.sem, 1)
                for c in range(DH):
                    pe.wait_ge(xc_ok.sem, xc_ok.at(b, c + 1))
                    ins = mm(bank[MISC][0:PR, :], w["x_proj_w"][:, c, :], xc[:, c, :], start=(c == 0), stop=(c == DH - 1))
                ins.then_inc(pr_mm.sem, 1)
                pe.wait_ge(pr_out.sem, pr_out.at(b, 1))
                pe.wait_ge(in_out.sem, in_out.at(b, 2 * DH))
                for c in range(DH):
                    mm(bank[HID_BANK[c]][:], w["dt_w"][:, c * P:(c + 1) * P], proj[:], start=True, stop=True
                       ).then_inc(dt_mm.sem, 1)
                pe.wait_ge(split_ok.sem, split_ok.at(b, 1))

                def add_state(n):
                    for c in range(DH):
                        pe.wait_ge(rd_ok.sem, rd_ok.at(b, DH * n + c + 1))
                        mm(bank[Y_BANK[c]][:], ident[:], read[:, n % 2, c, :], start=(n == 0), stop=(n == NS - 1)
                           ).then_inc(sum_mm.sem, 1)

                for n in range(NS):
                    if n >= 1:
                        pe.wait_ge(inj_ok.sem, inj_ok.at(b, DH * n))
                    mm(bank[BC_BANK[0]][:], select[:, n, :], split[:], start=True, stop=True).then_inc(b_mm.sem, 1)
                    if n >= 1:
                        pe.wait_ge(rd_ok.sem, rd_ok.at(b, DH * n))
                    mm(bank[BC_BANK[1]][:], select[:, NS + n, :], split[:], start=True, stop=True).then_inc(c_mm.sem, 1)
                    if n >= 1:
                        add_state(n - 1)
                add_state(NS - 1)
                pe.wait_ge(z_ok.sem, z_ok.at(b, DH))
                for t in range(NT):
                    for c in range(DH):
                        ins = mm(bank[OUT_BANK][:, t * P:(t + 1) * P], z[:, c, t * P:(t + 1) * P], w["out_w"][:, c, :],
                                 start=(c == 0), stop=(c == DH - 1))
                ins.then_inc(mix_mm.sem, 1)

                layernorm(b, 3, pr_out, pr_out.at(b, 1))
                router(b, 1, w["wg1"])

                def hid1(e):
                    for c in range(C1):
                        n = e * C1 + c
                        if n >= 2:
                            pe.wait_ge(hid1_act.sem, hid1_act.at(b, n - 1))
                        mm(bank[HID_BANK[n % 2]][:], w["w1"][:, e, c * P:(c + 1) * P], hT[3][:], start=True, stop=True
                           ).then_inc(hid1_mm.sem, 1)

                def out1(e):
                    pe.wait_ge(hid1_act.sem, hid1_act.at(b, (e + 1) * C1))
                    pe.wait_ge(out1_add.sem, out1_add.at(b, e + 1))
                    for t in range(NT):
                        for c in range(C1):
                            ins = mm(bank[OUT_BANK][:, t * P:(t + 1) * P],
                                     hidden[:, (e * C1 + c) % (2 * C1), t * P:(t + 1) * P],
                                     w["w2"][:, e * C1 + c, :], start=(c == 0), stop=(c == C1 - 1))
                    ins.then_inc(out1_mm.sem, 1)

                hid1(0)
                pe.wait_ge(gates_ok.sem, gates_ok.at(b, 2))
                for t in range(NT):
                    ins = tr(bank[MISC][0:E, t * P:(t + 1) * P], gates[:, t, :], ident[:])
                ins.then_inc(gt_mm.sem, 1)
                pe.wait_ge(gt_out.sem, gt_out.at(b, 1))
                for t in range(NT):
                    ins = mm(bank[OUT_BANK][:, t * P:(t + 1) * P], gates_T[:, t * P:(t + 1) * P], w["b2"][:],
                             start=True, stop=True)
                ins.then_inc(b2_mm.sem, 1)
                for e in range(1, E):
                    hid1(e)
                    out1(e - 1)
                out1(E - 1)

        @block.scalar
        def _(act):
            f = nc.scalar.activation
            act.wait_ge(weights_in, 16 * n_weights)
            f(silu_tanh[:], w["cT"][:], ACT.Tanh, scale=0.5).then_inc(setup_a, 1)
            f(a_exp[:], w["a_log"][:], ACT.Exp).then_inc(setup_a, 1)
            act.wait_ge(setup_p, 1)
            f(w_qk[:].rearrange("p g m -> p (g m)"), bank[0][:, 0:H * L], ACT.Copy, scale=SCALE).then_inc(setup_a, 1)
            f(w_vo[:].rearrange("p g m -> p (g m)"), bank[1][:, 0:G * P], ACT.Copy).then_inc(setup_a, 1)
            act.wait_ge(setup_v, SETUP_V)

            with act.Fori(0, B) as b:
                step = [0]

                def link(ins):
                    step[0] += 1
                    ins.then_inc(chain_a.sem, 1)
                    act.wait_ge(chain_a.sem, chain_a.at(b, step[0]))

                def layernorm(j, reader, n):
                    act.wait_ge(ln_var.sem, ln_var.at(b, j + 1))
                    link(f(log_var[:], meanvar[:, :, 1], ACT.Ln, bias=eps_col[:]))
                    f(rstd0[:], log_var[:], ACT.Exp, scale=-0.5).then_inc(ln_r0.sem, 1)
                    act.wait_ge(ln_T.sem, ln_T.at(b, j + 1))
                    l, k = j // 2, 3 * (j % 2)
                    f(hT[j][:], bank[MISC][:], ACT.Identity, bias=mod[:, l, k, bass.ds(b, 1)],
                      scale=mod[:, l, k + 1, bass.ds(b, 1)]).then_inc(h_ready.sem, 1)

                def route(layer):
                    act.wait_ge(gap_in.sem, gap_in.at(b, layer + 1))
                    f(gap_exp[:], gap[:], ACT.Exp).then_inc(gap_out.sem, 1)

                act.wait_ge(hid1_mm.sem, hid1_mm.before(b))
                layernorm(0, None, 0)
                for g in range(G):
                    act.wait_ge(q_mm.sem, q_mm.at(b, g + 1))
                    f(q_lat[:, g, :], bank[4 + g][:], ACT.Copy).then_inc(q_out.sem, 1)
                for n in range(UNITS):
                    g, i, pair = n // (2 * NT), n // 2 % NT, n % 2
                    act.wait_ge(s_max.sem, s_max.at(b, n + 1))
                    if n >= 2:
                        act.wait_ge(p_T.sem, p_T.at(b, 2 * n - 2))
                    for jj in range(2):
                        ins = f(probs[:, n % 2, jj, 0:(i + 1) * P], bank[2 * (n % 2) + jj][:, 0:(i + 1) * P], ACT.Exp,
                                bias=row_max[:, n % 2, jj:jj + 1],
                                accum_out=row_sum[:, g, i, 2 * pair + jj:2 * pair + jj + 1])
                    ins.then_inc(s_exp.sem, 1)
                    if n == UNITS // 2 + 2:
                        act.wait_ge(inv_mm.sem, inv_mm.at(b, 1))
                        f(inv_T[:], bank[MISC][:], ACT.Copy).then_inc(inv_out.sem, 1)
                act.wait_ge(inv_mm.sem, inv_mm.at(b, 2))
                act.wait_ge(y_out.sem, y_out.at(b, 1))
                f(inv_T[:], bank[MISC][:], ACT.Copy).then_inc(inv_out.sem, 1)

                layernorm(1, None, 0)
                route(0)
                for c in range(C0):
                    act.wait_ge(hid0_mm.sem, hid0_mm.at(b, c + 1))
                    if c == 0:
                        act.wait_ge(out1_mm.sem, out1_mm.before(b))
                    f(hidden[:, c, :], bank[HID_BANK[c % 2]][:], ACT.Gelu).then_inc(hid0_act.sem, 1)

                layernorm(2, None, 0)
                for c in range(2 * DH):
                    act.wait_ge(in_mm.sem, in_mm.at(b, c + 1))
                    to = xi[:, c, KC - 1:] if c < DH else res[:, c - DH, :]
                    f(to, bank[HID_BANK[c % 2]][:], ACT.Identity, bias=w["in_b"][:, c:c + 1]).then_inc(in_out.sem, 1)
                for c in range(DH):
                    act.wait_ge(conv_ok.sem, conv_ok.at(b, c + 1))
                    f(tanh_c[:, c, :], conv[1][:, c, :], ACT.Tanh, scale=0.5).then_inc(tanh_ok.sem, 1)
                act.wait_ge(xc_ok.sem, xc_ok.at(b, DH))
                act.wait_ge(in_out.sem, in_out.at(b, 2 * DH))
                for c in range(DH):
                    f(tanh_c[:, c, :], res[:, c, :], ACT.Tanh, scale=0.5).then_inc(tanh_ok.sem, 1)
                act.wait_ge(pr_mm.sem, pr_mm.at(b, 1))
                f(proj[:], bank[MISC][0:PR, :], ACT.Identity, bias=w["x_proj_b"][:]).then_inc(pr_out.sem, 1)
                for c in range(DH):
                    act.wait_ge(dt_z.sem, dt_z.at(b, c + 1))
                    link(f(dt_abs[:, c, :], dt_in[:, c, :], ACT.Abs))
                    link(f(dt_exp[:, c, :], dt_abs[:, c, :], ACT.Exp, scale=-1.0))
                    f(dt_log[:, c, :], dt_exp[:, c, :], ACT.Ln, bias=1.0).then_inc(dt_l.sem, 1)
                for n in range(NS):
                    for c in range(DH):
                        if n == 0:
                            act.wait_ge(delta_ok.sem, delta_ok.at(b, c + 1))
                        if n >= 4:
                            act.wait_ge(st_ok.sem, st_ok.at(b, (n - 4) * DH + c + 1))
                        f(decay[:, n % 4, c, :], delta[:, c, :], ACT.Exp, scale=a_neg[:, c, n:n + 1]
                          ).then_inc(dec_ok.sem, 1)

                layernorm(3, None, 0)
                route(1)
                act.wait_ge(hid0_gate.sem, hid0_gate.at(b, C0))
                for n in range(E * C1):
                    if n == C1:
                        act.wait_ge(gt_mm.sem, gt_mm.at(b, 1))
                        f(gates_T[:], bank[MISC][0:E, :], ACT.Copy).then_inc(gt_out.sem, 1)
                    act.wait_ge(hid1_mm.sem, hid1_mm.at(b, n + 1))
                    if n >= 2 * C1 and n % C1 == 0:
                        act.wait_ge(out1_mm.sem, out1_mm.at(b, n // C1 - 1))
                    f(hidden[:, n % (2 * C1), :], bank[HID_BANK[n % 2]][:], ACT.Gelu, bias=w["b1"][:, n:n + 1]
                      ).then_inc(hid1_act.sem, 1)
                assert step[0] == CHAIN_A_PER_BATCH, step[0]

        @block.vector
        def _(dve):
            v = nc.vector
            tt, ts, stt, cp = v.tensor_tensor, v.tensor_scalar, v.scalar_tensor_tensor, v.tensor_copy
            v.memset(eps_col[:], EPS)
            v.memset(xi[:], 0.0)
            v.memset(k_pad[:], 0.0)
            dve.wait_ge(weights_in, 16 * n_weights)
            cp(ident_bf[:], ident[:])
            cp(mask_bf[:], w["mask"][:])
            cp(select[:], w["stack"][:].unsqueeze(2).to_broadcast([3 * BC, BC, P]))
            ts(silu_half[:], w["cT"][:], 0.5, None, ALU.mult).then_inc(setup_v, 1)
            dve.wait_ge(setup_v, 1)
            dve.wait_ge(setup_a, 1)
            stt(silu_c[:], silu_tanh[:], 1.0, silu_half[:], ALU.add, ALU.mult).then_inc(setup_v, 1)
            dve.wait_ge(setup_v, 2)
            cp(silu_wide[:], silu_c[:].unsqueeze(3).to_broadcast([P, 2, B, P])).then_inc(setup_v, 1)
            dve.wait_ge(setup_a, 2)
            ts(a_neg[:], a_exp[:], -1.0, None, ALU.mult).then_inc(setup_v, 1)
            dve.wait_ge(setup_p, 1)
            cp(mod[:].rearrange("p l j b -> p (l j b)"), bank[2][:, 0:12 * B]).then_inc(setup_v, 1)
            dve.wait_ge(setup_v, 5)
            for k in (1, 4):
                ts(mod[:, :, k, :], mod[:, :, k, :], 1.0, None, ALU.add).then_inc(setup_v, 1)
            done = 7
            for b in range(B):
                dve.wait_ge(setup_p, 2 + b)
                g_row = bank[3 + b % 2][:].rearrange("p (k d) -> p k d", k=4)
                if b:
                    dve.wait_ge(setup_v, done)
                ts(gate_two[:], g_row, 0.0, 2.0, ALU.is_ge, ALU.mult).then_inc(setup_v2, 1)
                dve.wait_ge(setup_v2, 3 * b + 1)
                ts(gate_sign[:], gate_two[:], -1.0, None, ALU.add).then_inc(setup_v2, 1)
                dve.wait_ge(setup_v2, 3 * b + 2)
                tt(gate_size[:], g_row, gate_sign[:], ALU.mult).then_inc(setup_v2, 1)
                dve.wait_ge(setup_v2, 3 * b + 3)
                stt(gate[:, b, :, :], gate_size[:], 0.25, gate_sign[:], ALU.max, ALU.mult).then_inc(setup_v, 1)
                done += 1
            assert done == SETUP_V
            dve.wait_ge(setup_v, SETUP_V)

            with dve.Fori(0, B) as b:
                step = [0]

                def mark(ins):
                    step[0] += 1
                    ins.then_inc(chain.sem, 1)

                def sync():
                    dve.wait_ge(chain.sem, chain.at(b, step[0]))

                def link(ins):
                    mark(ins)
                    sync()

                def layernorm(j):
                    for t in range(NT):
                        ins = v.bn_stats(stats[:, t, :], x[:, t, :])
                    mark(ins)
                    sync()
                    v.memset(newton[:], 0.0)
                    for t in range(NT):
                        ins = v.bn_aggr(meanvar[:, t, :], stats[:, t, :])
                    ins.then_inc(ln_var.sem, 1)
                    dve.wait_ge(ln_var.sem, ln_var.at(b, j + 1))
                    mark(ts(var_eps[:], meanvar[:, :, 1], EPS, None, ALU.add))
                    dve.wait_ge(ln_r0.sem, ln_r0.at(b, j + 1))
                    link(tt(newton[:], rstd0[:], rstd0[:], ALU.mult))
                    link(tt(newton2[:], newton[:], var_eps[:], ALU.mult))
                    link(ts(newton3[:], newton2[:], -0.5, 1.5, ALU.mult, ALU.add))
                    link(tt(rstd[:], rstd0[:], newton3[:], ALU.mult))
                    link(stt(shift[:], meanvar[:, :, 0], -1.0, rstd[:], ALU.mult, ALU.mult))
                    for t in range(NT):
                        ins = ts(xn[:, t, :], x[:, t, :], rstd[:, t:t + 1], shift[:, t:t + 1], ALU.mult, ALU.add)
                    ins.then_inc(ln_xn.sem, 1)

                def add_mixed(k, source, to, done):
                    g_row = gate[:, bass.ds(b, 1), k, :].to_broadcast([P, NT, P])
                    link(tt(mixed[:], source, g_row, ALU.mult))
                    tt(to[:], x[:], mixed[:], ALU.add).then_inc(done.sem, 1)

                def route(layer):
                    wide = [P, NT, E]
                    dve.wait_ge(log_mm.sem, log_mm.at(b, layer + 1))
                    order = w["order"][:].unsqueeze(1).to_broadcast(wide)
                    link(cp(logits[:], bank[MISC][:, 0:NT * E].rearrange("p (t e) -> p t e", e=E)))
                    for k, (pick, values) in enumerate(((pick1, logits), (pick2, r_b))):
                        link(v.reduce_max(top[:, k, :], values[:], AX_X))
                        link(tt(r_a[:], values[:], top[:, k, :].unsqueeze(2).to_broadcast(wide), ALU.is_equal))
                        link(tt(r_a[:], r_a[:], order, ALU.mult))
                        link(v.reduce_max(best[:, k, :], r_a[:], AX_X))
                        link(tt(pick[:], r_a[:], best[:, k, :].unsqueeze(2).to_broadcast(wide), ALU.is_equal))
                        if k == 0:
                            link(stt(r_b[:], pick[:], FAR, logits[:], ALU.mult, ALU.add))
                    tt(gap[:], top[:, 1, :], top[:, 0, :], ALU.subtract).then_inc(gap_in.sem, 1)
                    dve.wait_ge(gap_out.sem, gap_out.at(b, layer + 1))
                    link(ts(gap_one[:], gap_exp[:], 1.0, None, ALU.add))
                    link(v.reciprocal(share1[:], gap_one[:]))
                    link(tt(share2[:], share1[:], gap_exp[:], ALU.mult))
                    mark(tt(r_a[:], pick1[:], share1[:].unsqueeze(2).to_broadcast(wide), ALU.mult))
                    link(tt(r_b[:], pick2[:], share2[:].unsqueeze(2).to_broadcast(wide), ALU.mult))
                    if layer == 0:
                        link(tt(gates[:], r_a[:], r_b[:], ALU.add))
                        cp(gates_wide[:].rearrange("p t e f -> p (t e) f"),
                           gates[:].rearrange("p t e -> p (t e)").unsqueeze(2).to_broadcast([P, NT * E, F0])
                           ).then_inc(gates_ok.sem, 1)
                    else:
                        tt(gates[:], r_a[:], r_b[:], ALU.add).then_inc(gates_ok.sem, 1)

                dve.wait_ge(x_loaded.sem, x_loaded.at(b, 16))
                cp(x[:], x_in[:]).then_inc(x_taken.sem, 1)
                dve.wait_ge(x_taken.sem, x_taken.at(b, 1))

                layernorm(0)
                for g in range(G):
                    dve.wait_ge(q_mm.sem, q_mm.at(b, G + g + 1))
                    for j in range(HG):
                        ins = cp(k_pad[j * L:(j + 1) * L, g, j, :], bank[2 + g][j * L:(j + 1) * L, :])
                    ins.then_inc(k_out.sem, 1)
                dve.wait_ge(v_mm.sem, v_mm.at(b, 1))
                cp(v_lat[:].rearrange("p t m -> p (t m)"), bank[OUT_BANK][:, 0:NT * G * L]).then_inc(v_out.sem, 1)

                def row_maximum(n):
                    i = n // 2 % NT
                    dve.wait_ge(s_mm.sem, s_mm.at(b, n + 1))
                    if n >= 2:
                        dve.wait_ge(s_exp.sem, s_exp.at(b, n - 1))
                    for jj in range(2):
                        ins = v.reduce_max(row_neg[:, n % 2, jj:jj + 1], bank[2 * (n % 2) + jj][:, 0:(i + 1) * P], AX_X)
                    link(ins)
                    ts(row_max[:, n % 2, :], row_neg[:, n % 2, :], -1.0, None, ALU.mult).then_inc(s_max.sem, 1)

                def take_transposed(n):
                    i, pair = n // 2 % NT, n % 2
                    for jj in range(2):
                        dve.wait_ge(p_T.sem, p_T.at(b, 2 * n + jj + 1))
                        if n == UNITS // 2 and jj == 0:
                            dve.wait_ge(y_mm.sem, y_mm.at(b, 1))
                        cp(probs_T[:, 2 * pair + jj, 0:i + 1, i * P:(i + 1) * P],
                           bank[4 + jj][:, 0:(i + 1) * P].rearrange("p (k q) -> p k q", q=P)).then_inc(p_out.sem, 1)

                def widen(g):
                    dve.wait_ge(s_exp.sem, s_exp.at(b, (g + 1) * 2 * NT))
                    link(v.reciprocal(row_inv[:], row_sum[:, g, :, :]))
                    cp(inv_wide[:].rearrange("p t h l -> p (t h) l"),
                       row_inv[:].rearrange("p t h -> p (t h)").unsqueeze(2).to_broadcast([P, NT * HG, L])
                       ).then_inc(inv_w.sem, 1)

                def normalise(g):
                    dve.wait_ge(inv_out.sem, inv_out.at(b, g + 1))
                    dve.wait_ge(y_mm.sem, y_mm.at(b, g + 1))
                    tt(y_T[:, g, :], bank[OUT_BANK][:], inv_T[:], ALU.mult).then_inc(y_out.sem, 1)

                row_maximum(0)
                for n in range(UNITS):
                    if n + 1 < UNITS:
                        row_maximum(n + 1)
                    if n == UNITS // 2:
                        widen(0)
                    if n == UNITS // 2 + 2:
                        normalise(0)
                    take_transposed(n)
                widen(1)
                normalise(1)
                dve.wait_ge(attn_mm.sem, attn_mm.at(b, 1))
                add_mixed(0, bank[MISC][:].rearrange("p (t d) -> p t d", d=P), x, attn_add)
                dve.wait_ge(attn_add.sem, attn_add.at(b, 1))

                layernorm(1)
                route(0)
                for c in range(C0):
                    dve.wait_ge(hid0_act.sem, hid0_act.at(b, c + 1))
                    dve.wait_ge(gT_mm.sem, gT_mm.at(b, c + 1))
                    tt(gated[:, c, :], hidden[:, c, :], bank[c % 2][:], ALU.mult).then_inc(hid0_gate.sem, 1)
                dve.wait_ge(out0_mm.sem, out0_mm.at(b, 1))
                add_mixed(1, bank[OUT_BANK][:].rearrange("p (t d) -> p t d", d=P), x, out0_add)
                dve.wait_ge(out0_add.sem, out0_add.at(b, 1))

                layernorm(2)
                for c in range(DH):
                    dve.wait_ge(in_out.sem, in_out.at(b, c + 1))
                    link(ts(conv[0][:, c, :], xi[:, c, 0:T], w["conv_w"][:, c, 0:1], w["conv_b"][:, c:c + 1],
                            ALU.mult, ALU.add))
                    for k in range(1, KC):
                        ins = stt(conv[k % 2][:, c, :], xi[:, c, k:k + T], w["conv_w"][:, c, k:k + 1],
                                  conv[(k - 1) % 2][:, c, :], ALU.mult, ALU.add)
                        if k < KC - 1:
                            link(ins)
                    ins.then_inc(conv_ok.sem, 1)
                for c in range(DH):
                    dve.wait_ge(conv_ok.sem, conv_ok.at(b, c + 1))
                    link(ts(conv[0][:, c, :], conv[1][:, c, :], 0.5, None, ALU.mult))
                    dve.wait_ge(tanh_ok.sem, tanh_ok.at(b, c + 1))
                    stt(xc[:, c, :], tanh_c[:, c, :], 1.0, conv[0][:, c, :], ALU.add, ALU.mult).then_inc(xc_ok.sem, 1)
                dve.wait_ge(xc_ok.sem, xc_ok.at(b, DH))
                for c in range(DH):
                    link(ts(conv[0][:, c, :], res[:, c, :], 0.5, None, ALU.mult))
                    dve.wait_ge(tanh_ok.sem, tanh_ok.at(b, DH + c + 1))
                    mark(stt(res_gate[:, c, :], tanh_c[:, c, :], 1.0, conv[0][:, c, :], ALU.add, ALU.mult))
                dve.wait_ge(pr_out.sem, pr_out.at(b, 1))
                link(cp(split[:], proj[0:3 * BC, :]))
                for lo, hi in ((L, 2 * L), (2 * L, 3 * L)):
                    link(tt(part[lo:hi, :], proj[lo:hi, :], split[lo:hi, :], ALU.subtract))
                    link(cp(split[lo:hi, :], part[lo:hi, :]))
                lo = 2 * L
                link(tt(part2[lo:lo + L, :], part[lo:lo + L, :], split[lo:lo + L, :], ALU.subtract))
                cp(split[lo:lo + L, :], part2[lo:lo + L, :]).then_inc(split_ok.sem, 1)
                for c in range(DH):
                    dve.wait_ge(dt_mm.sem, dt_mm.at(b, c + 1))
                    ts(dt_in[:, c, :], bank[HID_BANK[c]][:], w["dt_b"][:, c:c + 1], None, ALU.add).then_inc(dt_z.sem, 1)
                for c in range(DH):
                    dve.wait_ge(dt_z.sem, dt_z.at(b, c + 1))
                    dve.wait_ge(dt_l.sem, dt_l.at(b, c + 1))
                    stt(delta[:, c, :], dt_in[:, c, :], 0.0, dt_log[:, c, :], ALU.max, ALU.add).then_inc(delta_ok.sem, 1)
                    dve.wait_ge(delta_ok.sem, delta_ok.at(b, c + 1))
                    tt(u[:, c, :], delta[:, c, :], xc[:, c, :], ALU.mult).then_inc(u_ok.sem, 1)
                dve.wait_ge(u_ok.sem, u_ok.at(b, DH))

                def read_out(n):
                    dve.wait_ge(c_mm.sem, c_mm.at(b, n + 1))
                    for c in range(DH):
                        dve.wait_ge(st_ok.sem, st_ok.at(b, DH * n + c + 1))
                        if n >= 2:
                            dve.wait_ge(sum_mm.sem, sum_mm.at(b, DH * (n - 2) + c + 1))
                        tt(read[:, n % 2, c, :], state[:, n % 2, c, :], bank[BC_BANK[1]][:], ALU.mult
                           ).then_inc(rd_ok.sem, 1)

                for n in range(NS):
                    dve.wait_ge(b_mm.sem, b_mm.at(b, n + 1))
                    for c in range(DH):
                        tt(inject[:, n % 2, c, :], u[:, c, :], bank[BC_BANK[0]][:], ALU.mult).then_inc(inj_ok.sem, 1)
                    for c in range(DH):
                        dve.wait_ge(dec_ok.sem, dec_ok.at(b, DH * n + c + 1))
                        dve.wait_ge(inj_ok.sem, inj_ok.at(b, DH * n + c + 1))
                        if n >= 2:
                            dve.wait_ge(rd_ok.sem, rd_ok.at(b, DH * (n - 2) + c + 1))
                        v.tensor_tensor_scan(state[:, n % 2, c, :], decay[:, n % 4, c, :], inject[:, n % 2, c, :], 0.0,
                                             ALU.mult, ALU.add).then_inc(st_ok.sem, 1)
                    read_out(n)
                for c in range(DH):
                    dve.wait_ge(sum_mm.sem, sum_mm.at(b, DH * (NS - 1) + c + 1))
                    link(stt(y_skip[:, c, :], xc[:, c, :], w["d_skip"][:, c:c + 1], bank[Y_BANK[c]][:],
                             ALU.mult, ALU.add))
                    tt(z[:, c, :], y_skip[:, c, :], res_gate[:, c, :], ALU.mult).then_inc(z_ok.sem, 1)
                dve.wait_ge(mix_mm.sem, mix_mm.at(b, 1))
                link(tt(expert_sum[:], bank[OUT_BANK][:].rearrange("p (t d) -> p t d", d=P),
                        w["out_b"][:].unsqueeze(1).to_broadcast([P, NT, P]), ALU.add))
                add_mixed(2, expert_sum[:], x, mix_add)
                dve.wait_ge(mix_add.sem, mix_add.at(b, 1))

                layernorm(3)
                route(1)
                dve.wait_ge(b2_mm.sem, b2_mm.at(b, 1))
                cp(expert_sum[:].rearrange("p t d -> p (t d)"), bank[OUT_BANK][:]).then_inc(out1_add.sem, 1)
                for e in range(E):
                    dve.wait_ge(out1_mm.sem, out1_mm.at(b, e + 1))
                    dve.wait_ge(out1_add.sem, out1_add.at(b, e + 1))
                    for t in range(NT):
                        ins = stt(expert_sum[:, t, :], bank[OUT_BANK][:, t * P:(t + 1) * P], gates[:, t, e:e + 1],
                                  expert_sum[:, t, :], ALU.mult, ALU.add)
                    ins.then_inc(out1_add.sem, 1)
                dve.wait_ge(out1_add.sem, out1_add.at(b, E + 1))
                dve.wait_ge(x_sent.sem, x_sent.before(b))
                add_mixed(3, expert_sum[:], x_out, x_final)
                assert step[0] == CHAIN_PER_BATCH, step[0]


CHAIN_PER_BATCH = 106
CHAIN_A_PER_BATCH = 8
SETUP_V = 15
SETUP_A = 4


def _laid_out(a):
    c = lambda v: np.ascontiguousarray(v)
    g = {k: np.asarray(v) for k, v in a.items()}
    chunks = lambda v, n: c(v.reshape(n, P, -1).transpose(1, 0, 2))
    o = {"x": g["L0_attn_x"]}
    o["wqT"] = c(g["L0_attn_wq"].reshape(P, H, P).transpose(2, 1, 0))
    o["wk_upT"] = c(g["L0_attn_wk_up"].T)
    o["wv_upT"] = c(g["L0_attn_wv_up"].T)
    o["wk4"] = c(np.repeat(g["L0_attn_wk_down"].reshape(P, G, 1, L), HG, axis=2).reshape(P, G, HG * L))
    o["wv_down"] = g["L0_attn_wv_down"]
    o["wo"] = chunks(g["L0_attn_wo"], H)
    o["wg0"] = c(g["L0_ffn_w_gate"].T)
    o["wfcT"] = c(g["L0_ffn_w_fc"].reshape(E * F0, P).T)
    o["wprojT"] = chunks(g["L0_ffn_w_proj"].transpose(0, 2, 1).reshape(E * F0, P), C0)
    o["cT"] = c(np.stack([g["L0_c"].T, g["L1_c"].T], axis=1))
    o["wmod"] = c(np.stack([g["L0_wmod"], g["L1_wmod"]], axis=1))
    o["in_w"] = g["L1_attn_in_proj_w"]
    o["in_b"] = c(g["L1_attn_in_proj_b"].reshape(2 * DH, P).T)
    o["conv_w"] = c(g["L1_attn_conv_w"].reshape(KC, DH, P).transpose(2, 1, 0))
    o["conv_b"] = c(g["L1_attn_conv_b"].reshape(DH, P).T)
    order = np.concatenate([np.arange(NS, 3 * NS)] * 3 + [np.arange(NS)])
    o["x_proj_w"] = chunks(g["L1_attn_x_proj_w"][:, order], DH)
    o["x_proj_b"] = c(g["L1_attn_x_proj_b"][order].reshape(PR, 1))
    dt_w = np.zeros((PR, DI), np.float32)
    dt_w[3 * BC:] = g["L1_attn_dt_proj_w"]
    o["dt_w"] = dt_w
    o["dt_b"] = c(g["L1_attn_dt_proj_b"].reshape(DH, P).T)
    o["a_log"] = c(g["L1_attn_A_log"].reshape(DH, P, NS).transpose(1, 0, 2))
    o["d_skip"] = c(g["L1_attn_D_skip"].reshape(DH, P).T)
    o["out_w"] = chunks(g["L1_attn_out_proj_w"], DH)
    o["out_b"] = c(np.broadcast_to(g["L1_attn_out_proj_b"], (P, P)))
    o["wg1"] = g["L1_ffn_gate_w"]
    o["w1"] = c(g["L1_ffn_w1"].transpose(1, 0, 2))
    o["b1"] = c(g["L1_ffn_b1"].reshape(E * C1, P).T)
    o["w2"] = chunks(g["L1_ffn_w2"].reshape(E * F1, P), E * C1)
    o["b2"] = g["L1_ffn_b2"]
    o["ident"] = np.eye(P, dtype=np.float32)
    o["mask"] = np.triu(np.full((P, P), FAR, np.float32), 1)
    o["stack"] = np.tile(np.eye(BC, dtype=np.float32), (3, 1))
    o["order"] = c(np.broadcast_to(np.arange(E, 0, -1, dtype=np.float32), (P, E)))
    return o


def kernel(**inputs):
    import concourse.bacc as bacc
    from concourse.bass_utils import run_bass_kernel_spmd

    nc = bacc.Bacc("TRN2", target_bir_lowering=False, num_devices=1)
    arrays, io = {}, {}
    for name, a in _laid_out(inputs).items():
        a = np.ascontiguousarray(a)
        arrays[f"in_{name}_dram"] = a
        io[name] = nc.dram_tensor(f"in_{name}_dram", a.shape, mybir.dt.from_np(a.dtype), kind="ExternalInput").ap()
    out = nc.dram_tensor("out_0_dram", (B, T, P), F32, kind="ExternalOutput").ap()
    nc.disable_value_cache = True
    build(nc, io, out)
    r = run_bass_kernel_spmd(nc, [arrays], core_ids=[0])
    return r.results[0]["out_0_dram"]
```

```python
from contextlib import ExitStack

import numpy as np

import concourse.bass as bass
from concourse import mybir

F32 = mybir.dt.float32
BF16 = mybir.dt.bfloat16
ALU = mybir.AluOpType
ACT = mybir.ActivationFunctionType
AX_X = mybir.AxisListType.X

P = 128
B = 8
T = 512
NT = T // P
H = 8
G = 2
HG = H // G
L = 32
E = 8
F0 = 64
C0 = E * F0 // P
F1 = 512
C1 = F1 // P
DI = 256
DH = DI // P
NS = 16
KC = 4
BC = 2 * NS
PR = 3 * BC + NS
EPS = 1e-5
SCALE = float(P) ** -0.5
FAR = -3.0e38


class Signal:

    def __init__(self, sem, per_batch, primed):
        self.sem, self.per_batch, self.primed = sem, per_batch, primed

    def at(self, b, n):
        return b * self.per_batch + n + self.primed

    def before(self, b):
        assert self.primed
        return b * self.per_batch + self.primed


def build(nc, io, out):
    ctx = ExitStack()
    with ctx:
        def sb(name, shape, dt=F32):
            return ctx.enter_context(nc.sbuf_tensor(name, shape, dt))

        def sem(name):
            return ctx.enter_context(nc.semaphore(name))

        def signal(name, per_batch, primed=0):
            return Signal(sem(name), per_batch, primed)

        probs_T = sb("probs_T", [P, HG, NT, T])
        setup_space = probs_T[:].rearrange("p h k q -> p (h k q)")
        setup_only = {"wqT": 0, "wo": H * P, "wmod": 2 * H * P}
        w = {name: sb("w_" + name, list(ap.shape)) for name, ap in io.items() if name not in ("x", *setup_only)}
        w["wqT"] = setup_space[:, 0:H * P].rearrange("p (h d) -> p h d", h=H)
        w["wo"] = setup_space[:, H * P:2 * H * P].rearrange("p (h d) -> p h d", h=H)
        w["wmod"] = setup_space[:, 2 * H * P:2 * H * P + 12 * P].rearrange("p (l d) -> p l d", l=2)
        silu_wide = setup_space[:, 4 * H * P:4 * H * P + 2 * B * P].rearrange("p (l b d) -> p l b d", l=2, b=B)
        ident = w["ident"]

        ident_bf = sb("ident_bf", [P, P], BF16)
        mask_bf = sb("mask_bf", [P, P], BF16)
        select = sb("select", [3 * BC, BC, P], BF16)
        silu_c = sb("silu_c", [P, 2, B])
        silu_half = sb("silu_half", [P, 2, B])
        silu_tanh = sb("silu_tanh", [P, 2, B])
        mod = sb("mod", [P, 2, 6, B])
        gate = sb("gate", [P, B, 4, P])
        gate_sign = sb("gate_sign", [P, 4, P])
        gate_size = sb("gate_size", [P, 4, P])
        gate_two = sb("gate_two", [P, 4, P])
        w_qk = sb("w_qk", [P, G, HG * L])
        w_vo = sb("w_vo", [P, G, P])
        a_neg = sb("a_neg", [P, DH, NS])
        a_exp = sb("a_exp", [P, DH, NS])
        eps_col = sb("eps_col", [P, 1])

        x_in = sb("x_in", [P, NT, P])
        x = sb("x", [P, NT, P])
        x_out = sb("x_out", [P, NT, P])
        mixed = sb("mixed", [P, NT, P])
        x_mid = sb("x_mid", [P, NT, P])
        expert_out = sb("expert_out", [P, NT, P])
        mixer_out = sb("mixer_out", [P, NT, P])
        stats = sb("stats", [P, NT, 6])
        meanvar = sb("meanvar", [P, NT, 2])
        log_var = sb("log_var", [P, NT])
        rstd0 = sb("rstd0", [P, NT])
        var_eps = sb("var_eps", [P, NT])
        newton = sb("newton", [P, NT])
        newton2 = sb("newton2", [P, NT])
        newton3 = sb("newton3", [P, NT])
        rstd = sb("rstd", [P, NT])
        shift = sb("shift", [P, NT])
        xn = sb("xn", [P, NT, P])
        hT = [sb(f"hT{j}", [P, T]) for j in range(4)]

        hidden = sb("hidden", [P, 2 * C1, T])
        q_lat = hidden[:, 0:G, :]
        k_pad = sb("k_pad", [P, G, HG, T])
        v_lat = hidden[:, 6, 0:NT * G * L].rearrange("p (t m) -> p t m", t=NT)
        row_neg = sb("row_neg", [P, 2, 2])
        row_max = sb("row_max", [P, 2, 2])
        probs = sb("probs", [P, 2, 2, T])
        row_sum = sb("row_sum", [P, G, NT, HG])
        row_inv = sb("row_inv", [P, NT, HG])
        inv_wide = hidden[:, 4, :].rearrange("p (t h l) -> p t h l", t=NT, h=HG)
        inv_T = hidden[:, 5, :]
        y_T = hidden[:, G:2 * G, :]

        logits = sb("logits", [P, NT, E])
        r_a = sb("r_a", [P, NT, E])
        r_b = sb("r_b", [P, NT, E])
        top = sb("top", [P, 2, NT])
        best = sb("best", [P, 2, NT])
        pick1 = sb("pick1", [P, NT, E])
        pick2 = sb("pick2", [P, NT, E])
        gap = sb("gap", [P, NT])
        gap_exp = sb("gap_exp", [P, NT])
        gap_one = sb("gap_one", [P, NT])
        share1 = sb("share1", [P, NT])
        share2 = sb("share2", [P, NT])
        gates = [sb(f"gates{l}", [P, NT, E]) for l in range(2)]
        gates_wide = probs[:].rearrange("p a b (c f) -> p (a b) c f", f=F0)
        gates_T = sb("gates_T", [E, T])

        gated = hidden[:, C1:2 * C1, :]
        expert_sum = sb("expert_sum", [P, NT, P])

        xi = sb("xi", [P, DH, T + KC - 1])
        mix_space = probs_T[:].rearrange("p h k q -> p (h k q)")

        def within(first, *shape):
            n = int(np.prod(shape))
            flat = mix_space[:, first * T:(first + n) * T]
            if len(shape) == 1:
                return flat.rearrange("p (a t) -> p a t", a=shape[0])
            return flat.rearrange("p (a c t) -> p a c t", a=shape[0], c=shape[1])

        decay = within(0, 4, DH)
        inject = within(8, 2, DH)
        state = within(12, 2, DH)
        read = probs
        conv = [within(0, DH), within(DH, DH)]
        tanh_c = within(8, DH)
        res = within(12, DH)
        part = mix_space[0:3 * BC, 14 * T:15 * T]
        part2 = mix_space[0:3 * BC, 15 * T:16 * T]
        dt_exp, dt_abs, dt_log, z, y_skip = conv[0], conv[1], tanh_c, conv[0], conv[1]
        xc = sb("xc", [P, DH, T])
        res_gate = sb("res_gate", [P, DH, T])
        proj = sb("proj", [PR, T])
        split = sb("split", [3 * BC, T], BF16)
        dt_in = sb("dt_in", [P, DH, T])
        delta = sb("delta", [P, DH, T])
        u = sb("u", [P, DH, T])
        state_sum = dt_in

        bank = [ctx.enter_context(nc.psum_tensor(f"bank{i}", [P, T], F32)) for i in range(8)]
        score = [ctx.enter_context(nc.psum_tensor(f"score{i}", [P, 2, T], F32)) for i in range(0)]
        BC_BANK, HID0_BANK, HID_BANK, OUT_BANK, MISC = (0, 1), (4, 5), (2, 3, 4, 5), 6, 7
        OUT1_BANK = (6, 7)

        weights_in = sem("weights_in")
        setup_v, setup_a, setup_p, setup_v2 = sem("setup_v"), sem("setup_a"), sem("setup_p"), sem("setup_v2")
        x_loaded = signal("x_loaded", 16)
        x_stored = signal("x_stored", 16)
        x_sent = signal("x_sent", 1, primed=1)
        x_taken = signal("x_taken", 1, primed=1)
        x_final = signal("x_final", 1)
        chain = signal("chain", CHAIN_PER_BATCH)
        chain_a = signal("chain_a", CHAIN_A_PER_BATCH)
        ln_var = signal("ln_var", 4)
        ln_r0 = signal("ln_r0", 4)
        ln_xn = signal("ln_xn", 4)
        ln_T = signal("ln_T", 4)
        h_ready = signal("h_ready", 4)

        q_mm = signal("q_mm", 2 * G)
        q_out = signal("q_out", G)
        k_out = signal("k_out", G)
        v_mm = signal("v_mm", 1)
        v_out = signal("v_out", 1)
        UNITS = G * NT * 2
        s_mm = signal("s_mm", UNITS)
        s_max = signal("s_max", UNITS)
        s_exp = signal("s_exp", UNITS)
        p_T = signal("p_T", 2 * UNITS)
        p_out = signal("p_out", 2 * UNITS)
        y_mm = signal("y_mm", G)
        inv_w = signal("inv_w", G)
        inv_mm = signal("inv_mm", G)
        inv_out = signal("inv_out", G)
        y_out = signal("y_out", G)
        attn_mm = signal("attn_mm", 1)
        attn_add = signal("attn_add", 1)

        log_mm = signal("log_mm", 2)
        gap_in = signal("gap_in", 2)
        gap_out = signal("gap_out", 2)
        gates_ok = signal("gates_ok", 2)
        hid0_mm = signal("hid0_mm", C0)
        hid0_act = signal("hid0_act", C0)
        gT_mm = signal("gT_mm", C0)
        hid0_gate = signal("hid0_gate", C0)
        out0_mm = signal("out0_mm", 1)
        out0_add = signal("out0_add", 1)

        in_mm = signal("in_mm", 2 * DH)
        in_out = signal("in_out", 2 * DH)
        conv_ok = signal("conv_ok", DH)
        tanh_ok = signal("tanh_ok", 2 * DH)
        xc_ok = signal("xc_ok", DH)
        pr_mm = signal("pr_mm", 1)
        pr_out = signal("pr_out", 1)
        split_ok = signal("split_ok", 1)
        dt_mm = signal("dt_mm", DH)
        dt_z = signal("dt_z", DH)
        dt_l = signal("dt_l", DH)
        delta_ok = signal("delta_ok", DH)
        u_ok = signal("u_ok", DH)
        dec_ok = signal("dec_ok", NS * DH)
        b_mm = signal("b_mm", NS)
        c_mm = signal("c_mm", NS)
        inj_ok = signal("inj_ok", NS)
        st_ok = signal("st_ok", NS * DH)
        rd_ok = signal("rd_ok", NS)
        acc_ok = signal("acc_ok", NS - 1)
        z_ok = signal("z_ok", DH)
        mix_mm = signal("mix_mm", 1)
        mix_add = signal("mix_add", 1)

        gt_mm = signal("gt_mm", 1)
        gt_out = signal("gt_out", 1)
        b2_mm = signal("b2_mm", 1)
        hid1_mm = signal("hid1_mm", E * C1)
        hid1_act = signal("hid1_act", E * C1)
        out1_mm = signal("out1_mm", E * NT)
        out1_add = signal("out1_add", E * NT + 1)
        out1_gate = signal("out1_gate", 1)

        n_weights = len(w)
        block = ctx.enter_context(nc.Block())

        @block.sync
        def _(sp):
            for name, tile in w.items():
                sp.dma_start(tile[:], io[name]).then_inc(weights_in, 16)
            for s in (x_sent, x_taken):
                sp.sem_inc(s.sem, 1)

        @block.gpsimd
        def _(pool):
            x_rows = io["x"].rearrange("b (t p) d -> b p t d", p=P)
            out_rows = out.rearrange("b (t p) d -> b p t d", p=P)

            def load(b):
                pool.wait_ge(x_taken.sem, x_taken.before(b))
                pool.dma_start(x_in[:], x_rows[bass.ds(b, 1), :, :, :].rearrange("a p t d -> p (a t) d")
                               ).then_inc(x_loaded.sem, 16)

            def store(b):
                pool.wait_ge(x_final.sem, x_final.at(b, 1))
                pool.dma_start(out_rows[bass.ds(b, 1), :, :, :].rearrange("a p t d -> p (a t) d"), x_out[:]
                               ).then_inc(x_stored.sem, 16)
                pool.wait_ge(x_stored.sem, x_stored.at(b, 16))
                pool.sem_inc(x_sent.sem, 1)

            def sum_states(b):
                for n in range(1, NS):
                    pool.wait_ge(rd_ok.sem, rd_ok.at(b, n + 1))
                    if n == 1:
                        ins = nc.gpsimd.tensor_tensor(state_sum[:], read[:, 0, :, :], read[:, 1, :, :], ALU.add)
                    else:
                        pool.wait_ge(acc_ok.sem, acc_ok.at(b, n - 1))
                        ins = nc.gpsimd.tensor_tensor(state_sum[:], state_sum[:], read[:, n % 2, :, :], ALU.add)
                    ins.then_inc(acc_ok.sem, 1)

            load(0)
            sum_states(0)
            with pool.Fori(1, B) as b:
                load(b)
                sum_states(b)
                store(b - 1)
            store(B - 1)

        @block.tensor
        def _(pe):
            mm, tr = nc.tensor.matmul, nc.tensor.transpose

            pe.wait_ge(weights_in, 16 * n_weights)
            for h in range(H):
                ins = mm(bank[0][:, h * L:(h + 1) * L], w["wqT"][:, h, :], w["wk_upT"][:], start=True, stop=True)
            for h in range(H):
                g, j = divmod(h, HG)
                ins = mm(bank[1][j * L:(j + 1) * L, g * P:(g + 1) * P], w["wv_upT"][:], w["wo"][:, h, :],
                         start=True, stop=True)
            pe.wait_ge(setup_v, 3)
            for l in range(2):
                for j in range(6):
                    ins = mm(bank[2][:, (l * 6 + j) * B:(l * 6 + j + 1) * B], w["wmod"][:, l, j * P:(j + 1) * P],
                             silu_c[:, l, :], start=True, stop=True)
            ins.then_inc(setup_p, 1)
            for b in range(B):
                if b >= 2:
                    pe.wait_ge(setup_v, 7 + b - 1)
                for k in range(4):
                    l, j = k // 2, 2 if k % 2 == 0 else 5
                    ins = mm(bank[3 + b % 2][:, k * P:(k + 1) * P], silu_wide[:, l, b, :],
                             w["wmod"][:, l, j * P:(j + 1) * P], start=True, stop=True)
                ins.then_inc(setup_p, 1)
            pe.wait_ge(setup_v, SETUP_V)
            pe.wait_ge(setup_a, SETUP_A)

            def layernorm(b, j, free, value):
                pe.wait_ge(ln_xn.sem, ln_xn.at(b, j + 1))
                pe.wait_ge(free.sem, value)
                for t in range(NT):
                    ins = tr(bank[MISC][:, t * P:(t + 1) * P], xn[:, t, :], ident[:])
                ins.then_inc(ln_T.sem, 1)
                pe.wait_ge(h_ready.sem, h_ready.at(b, j + 1))

            def router(b, layer, weight):
                for t in range(NT):
                    ins = mm(bank[MISC][:, t * E:(t + 1) * E], hT[2 * layer + 1][:, t * P:(t + 1) * P], weight[:],
                             start=True, stop=True)
                ins.then_inc(log_mm.sem, 1)

            def hid1(b, n):
                if n >= 4:
                    pe.wait_ge(hid1_act.sem, hid1_act.at(b, n - 3))
                mm(bank[HID_BANK[n % 4]][:], w["w1"][:, n // C1, n % C1 * P:(n % C1 + 1) * P], hT[3][:],
                   start=True, stop=True).then_inc(hid1_mm.sem, 1)

            def out1(b, n):
                e, t = divmod(n, NT)
                if t == 0:
                    pe.wait_ge(hid1_act.sem, hid1_act.at(b, (e + 1) * C1))
                    if e != 1:
                        pe.wait_ge(out1_add.sem, out1_add.at(b, max(e - 1, 0) * NT + 1))
                for c in range(C1):
                    ins = mm(bank[OUT1_BANK[e % 2]][:, t * P:(t + 1) * P], hidden[:, (e * C1 + c) % (2 * C1), t * P:(t + 1) * P],
                             w["w2"][:, e * C1 + c, :], start=(c == 0), stop=(c == C1 - 1))
                ins.then_inc(out1_mm.sem, 1)

            def iteration(b, experts):
                layernorm(b, 0, x_taken, x_taken.at(b, 1))
                for g in range(G):
                    pe_bank = bank[4 + g]
                    mm(pe_bank[:], w_qk[:, g, :], hT[0][:], start=True, stop=True).then_inc(q_mm.sem, 1)
                for g in range(G):
                    mm(bank[2 + g][:], w["wk4"][:, g, :], hT[0][:], start=True, stop=True).then_inc(q_mm.sem, 1)
                if experts:
                    pe.wait_ge(out1_add.sem, out1_add.at(b - 1, 1))
                for t in range(NT):
                    ins = mm(bank[OUT_BANK][:, t * G * L:(t + 1) * G * L], hT[0][:, t * P:(t + 1) * P], w["wv_down"][:],
                             start=True, stop=True)
                ins.then_inc(v_mm.sem, 1)

                def scores(n):
                    g, i, pair = n // (2 * NT), n // 2 % NT, n % 2
                    if i == 0 and pair == 0:
                        pe.wait_ge(q_out.sem, q_out.at(b, g + 1))
                        pe.wait_ge(k_out.sem, k_out.at(b, g + 1))
                    if n == 1:
                        pe.wait_ge(k_out.sem, k_out.at(b, G))
                    if n >= 2:
                        pe.wait_ge(s_exp.sem, s_exp.at(b, n - 1))
                    for jj in range(2):
                        j = 2 * pair + jj
                        s = bank[2 * (n % 2) + jj]
                        mm(s[:, 0:(i + 1) * P], q_lat[:, g, i * P:(i + 1) * P], k_pad[:, g, j, 0:(i + 1) * P],
                           start=True, stop=False)
                        ins = mm(s[:, i * P:(i + 1) * P], ident_bf[:], mask_bf[:], start=False, stop=True)
                    ins.then_inc(s_mm.sem, 1)

                def transposes(n):
                    i = n // 2 % NT
                    pe.wait_ge(s_exp.sem, s_exp.at(b, n + 1))
                    for jj in range(2):
                        if n == 0:
                            pe.wait_ge(q_out.sem, q_out.at(b, G))
                        else:
                            pe.wait_ge(p_out.sem, p_out.at(b, 2 * n + jj - 1))
                        for k in range(i + 1):
                            ins = tr(bank[4 + jj][:, k * P:(k + 1) * P], probs[:, n % 2, jj, k * P:(k + 1) * P], ident[:])
                        ins.then_inc(p_T.sem, 1)

                def values(g):
                    pe.wait_ge(p_out.sem, p_out.at(b, (g + 1) * 4 * NT))
                    pe.wait_ge(v_out.sem, v_out.at(b, 1))
                    if g > 0:
                        pe.wait_ge(y_out.sem, y_out.at(b, g))
                    for k in range(NT):
                        for j in range(HG):
                            ins = mm(bank[OUT_BANK][j * L:(j + 1) * L, k * P:T], v_lat[:, k, g * L:(g + 1) * L],
                                     probs_T[:, j, k, k * P:T], start=(k == 0), stop=(k == NT - 1),
                                     skip_group_check=True)
                    ins.then_inc(y_mm.sem, 1)
                    pe.wait_ge(inv_w.sem, inv_w.at(b, g + 1))
                    for t in range(NT):
                        ins = tr(bank[MISC][:, t * P:(t + 1) * P], inv_wide[:, t, :, :].rearrange("p h l -> p (h l)"),
                                 ident[:])
                    ins.then_inc(inv_mm.sem, 1)

                for n in range(UNITS + 1):
                    if n < UNITS:
                        scores(n)
                    if n >= 1:
                        transposes(n - 1)
                    if n == UNITS // 2 + 1:
                        values(0)
                values(1)
                pe.wait_ge(y_out.sem, y_out.at(b, G))
                for t in range(NT):
                    for g in range(G):
                        ins = mm(bank[MISC][:, t * P:(t + 1) * P], y_T[:, g, t * P:(t + 1) * P], w_vo[:, g, :],
                                 start=(g == 0), stop=(g == G - 1))
                ins.then_inc(attn_mm.sem, 1)

                layernorm(b, 1, attn_add, attn_add.at(b, 1))
                router(b, 0, w["wg0"])
                for c in range(C0):
                    if c >= 2:
                        pe.wait_ge(hid0_act.sem, hid0_act.at(b, c - 1))
                    mm(bank[HID0_BANK[c % 2]][:], w["wfcT"][:, c * P:(c + 1) * P], hT[1][:], start=True, stop=True
                       ).then_inc(hid0_mm.sem, 1)
                pe.wait_ge(gates_ok.sem, gates_ok.at(b, 1))
                for c in range(C0):
                    if c >= 2:
                        pe.wait_ge(hid0_gate.sem, hid0_gate.at(b, c - 1))
                    for t in range(NT):
                        wide = gates_wide[:, t, :, :].rearrange("p e f -> p (e f)")
                        ins = tr(bank[c % 2][:, t * P:(t + 1) * P], wide[:, c * P:(c + 1) * P], ident[:])
                    ins.then_inc(gT_mm.sem, 1)
                pe.wait_ge(hid0_gate.sem, hid0_gate.at(b, C0))
                for t in range(NT):
                    for c in range(C0):
                        ins = mm(bank[OUT_BANK][:, t * P:(t + 1) * P], gated[:, c, t * P:(t + 1) * P],
                                 w["wprojT"][:, c, :], start=(c == 0), stop=(c == C0 - 1))
                ins.then_inc(out0_mm.sem, 1)

                layernorm(b, 2, gates_ok, gates_ok.at(b, 1))
                for c in range(2 * DH):
                    if c >= 2:
                        pe.wait_ge(in_out.sem, in_out.at(b, c - 1))
                    mm(bank[HID0_BANK[c % 2]][:], w["in_w"][:, c * P:(c + 1) * P], hT[2][:], start=True, stop=True
                       ).then_inc(in_mm.sem, 1)
                for c in range(DH):
                    pe.wait_ge(xc_ok.sem, xc_ok.at(b, c + 1))
                    ins = mm(bank[MISC][0:PR, :], w["x_proj_w"][:, c, :], xc[:, c, :], start=(c == 0), stop=(c == DH - 1))
                ins.then_inc(pr_mm.sem, 1)
                pe.wait_ge(pr_out.sem, pr_out.at(b, 1))
                pe.wait_ge(in_out.sem, in_out.at(b, 2 * DH))
                for c in range(DH):
                    mm(bank[HID0_BANK[c]][:], w["dt_w"][:, c * P:(c + 1) * P], proj[:], start=True, stop=True
                       ).then_inc(dt_mm.sem, 1)
                pe.wait_ge(split_ok.sem, split_ok.at(b, 1))

                pe.wait_ge(dt_z.sem, dt_z.at(b, DH))

                def spread_b(n):
                    if n >= 1:
                        pe.wait_ge(inj_ok.sem, inj_ok.at(b, n))
                    mm(bank[BC_BANK[0]][:], select[:, n, :], split[:], start=True, stop=True).then_inc(b_mm.sem, 1)

                def expert_piece(n, k):
                    if experts:
                        (hid1 if n % 4 < 2 else out1)(b - 1, 8 * (n // 4) + 4 * (n % 2) + k)

                spread_b(0)
                spread_b(1)
                for n in range(NS):
                    if n >= 1:
                        pe.wait_ge(rd_ok.sem, rd_ok.at(b, n))
                    mm(bank[BC_BANK[1]][:], select[:, NS + n, :], split[:], start=True, stop=True).then_inc(c_mm.sem, 1)
                    expert_piece(n, 0)
                    if n + 2 < NS:
                        spread_b(n + 2)
                    for k in range(1, 4):
                        expert_piece(n, k)
                pe.wait_ge(z_ok.sem, z_ok.at(b, DH))
                for t in range(NT):
                    for c in range(DH):
                        ins = mm(bank[OUT_BANK][:, t * P:(t + 1) * P], z[:, c, t * P:(t + 1) * P], w["out_w"][:, c, :],
                                 start=(c == 0), stop=(c == DH - 1))
                ins.then_inc(mix_mm.sem, 1)

                layernorm(b, 3, pr_out, pr_out.at(b, 1))
                router(b, 1, w["wg1"])

                pe.wait_ge(gates_ok.sem, gates_ok.at(b, 2))
                for t in range(NT):
                    ins = tr(bank[MISC][0:E, t * P:(t + 1) * P], gates[1][:, t, :], ident[:])
                ins.then_inc(gt_mm.sem, 1)
                pe.wait_ge(gt_out.sem, gt_out.at(b, 1))
                for t in range(NT):
                    ins = mm(bank[OUT_BANK][:, t * P:(t + 1) * P], gates_T[:, t * P:(t + 1) * P], w["b2"][:],
                             start=True, stop=True)
                ins.then_inc(b2_mm.sem, 1)

            iteration(0, False)
            with pe.Fori(1, B) as b:
                iteration(b, True)
            for k in range(4):
                for n in range(2 * C1):
                    hid1(B - 1, 2 * C1 * k + n)
                for n in range(2 * NT):
                    out1(B - 1, 2 * NT * k + n)

        @block.scalar
        def _(act):
            f = nc.scalar.activation
            act.wait_ge(weights_in, 16 * n_weights)
            f(silu_tanh[:], w["cT"][:], ACT.Tanh, scale=0.5).then_inc(setup_a, 1)
            f(a_exp[:], w["a_log"][:], ACT.Exp).then_inc(setup_a, 1)
            act.wait_ge(setup_p, 1)
            f(w_qk[:].rearrange("p g m -> p (g m)"), bank[0][:, 0:H * L], ACT.Copy, scale=SCALE).then_inc(setup_a, 1)
            f(w_vo[:].rearrange("p g m -> p (g m)"), bank[1][:, 0:G * P], ACT.Copy).then_inc(setup_a, 1)
            act.wait_ge(setup_v, SETUP_V)

            def gelu1(b, n):
                act.wait_ge(hid1_mm.sem, hid1_mm.at(b, n + 1))
                if n >= 2 * C1 and n % C1 == 0:
                    act.wait_ge(out1_mm.sem, out1_mm.at(b, NT * (n // C1 - 1)))
                f(hidden[:, n % (2 * C1), :], bank[HID_BANK[n % 4]][:], ACT.Gelu, bias=w["b1"][:, n:n + 1]
                  ).then_inc(hid1_act.sem, 1)

            def iteration(b, experts):
                step = [0]

                def link(ins):
                    step[0] += 1
                    ins.then_inc(chain_a.sem, 1)
                    act.wait_ge(chain_a.sem, chain_a.at(b, step[0]))

                def layernorm(j, reader, n):
                    act.wait_ge(ln_var.sem, ln_var.at(b, j + 1))
                    link(f(log_var[:], meanvar[:, :, 1], ACT.Ln, bias=eps_col[:]))
                    f(rstd0[:], log_var[:], ACT.Exp, scale=-0.5).then_inc(ln_r0.sem, 1)
                    act.wait_ge(ln_T.sem, ln_T.at(b, j + 1))
                    l, k = j // 2, 3 * (j % 2)
                    f(hT[j][:], bank[MISC][:], ACT.Identity, bias=mod[:, l, k, bass.ds(b, 1)],
                      scale=mod[:, l, k + 1, bass.ds(b, 1)]).then_inc(h_ready.sem, 1)

                def route(layer):
                    act.wait_ge(gap_in.sem, gap_in.at(b, layer + 1))
                    f(gap_exp[:], gap[:], ACT.Exp).then_inc(gap_out.sem, 1)

                layernorm(0, None, 0)
                for g in range(G):
                    act.wait_ge(q_mm.sem, q_mm.at(b, g + 1))
                    f(q_lat[:, g, :], bank[4 + g][:], ACT.Copy).then_inc(q_out.sem, 1)
                for n in range(UNITS):
                    g, i, pair = n // (2 * NT), n // 2 % NT, n % 2
                    act.wait_ge(s_max.sem, s_max.at(b, n + 1))
                    if n >= 2:
                        act.wait_ge(p_T.sem, p_T.at(b, 2 * n - 2))
                    for jj in range(2):
                        ins = f(probs[:, n % 2, jj, 0:(i + 1) * P], bank[2 * (n % 2) + jj][:, 0:(i + 1) * P], ACT.Exp,
                                bias=row_max[:, n % 2, jj:jj + 1],
                                accum_out=row_sum[:, g, i, 2 * pair + jj:2 * pair + jj + 1])
                    ins.then_inc(s_exp.sem, 1)
                    if n == UNITS // 2 + 2:
                        act.wait_ge(inv_mm.sem, inv_mm.at(b, 1))
                        f(inv_T[:], bank[MISC][:], ACT.Copy).then_inc(inv_out.sem, 1)
                act.wait_ge(inv_mm.sem, inv_mm.at(b, 2))
                act.wait_ge(y_out.sem, y_out.at(b, 1))
                f(inv_T[:], bank[MISC][:], ACT.Copy).then_inc(inv_out.sem, 1)

                layernorm(1, None, 0)
                route(0)
                for c in range(C0):
                    act.wait_ge(hid0_mm.sem, hid0_mm.at(b, c + 1))
                    f(hidden[:, c, :], bank[HID0_BANK[c % 2]][:], ACT.Gelu).then_inc(hid0_act.sem, 1)

                layernorm(2, None, 0)
                for c in range(2 * DH):
                    act.wait_ge(in_mm.sem, in_mm.at(b, c + 1))
                    to = xi[:, c, KC - 1:] if c < DH else res[:, c - DH, :]
                    f(to, bank[HID0_BANK[c % 2]][:], ACT.Identity, bias=w["in_b"][:, c:c + 1]).then_inc(in_out.sem, 1)
                for c in range(DH):
                    act.wait_ge(conv_ok.sem, conv_ok.at(b, c + 1))
                    f(tanh_c[:, c, :], conv[1][:, c, :], ACT.Tanh, scale=0.5).then_inc(tanh_ok.sem, 1)
                act.wait_ge(xc_ok.sem, xc_ok.at(b, DH))
                act.wait_ge(in_out.sem, in_out.at(b, 2 * DH))
                for c in range(DH):
                    f(tanh_c[:, c, :], res[:, c, :], ACT.Tanh, scale=0.5).then_inc(tanh_ok.sem, 1)
                act.wait_ge(pr_mm.sem, pr_mm.at(b, 1))
                f(proj[:], bank[MISC][0:PR, :], ACT.Identity, bias=w["x_proj_b"][:]).then_inc(pr_out.sem, 1)
                for c in range(DH):
                    act.wait_ge(dt_z.sem, dt_z.at(b, c + 1))
                    link(f(dt_abs[:, c, :], dt_in[:, c, :], ACT.Abs))
                    link(f(dt_exp[:, c, :], dt_abs[:, c, :], ACT.Exp, scale=-1.0))
                    f(dt_log[:, c, :], dt_exp[:, c, :], ACT.Ln, bias=1.0).then_inc(dt_l.sem, 1)
                def decays(n):
                    for c in range(DH):
                        if n >= 4:
                            act.wait_ge(st_ok.sem, st_ok.at(b, (n - 4) * DH + c + 1))
                        f(decay[:, n % 4, c, :], delta[:, c, :], ACT.Exp, scale=a_neg[:, c, n:n + 1]
                          ).then_inc(dec_ok.sem, 1)

                act.wait_ge(delta_ok.sem, delta_ok.at(b, DH))
                for n in range(4):
                    decays(n)
                for k in range(NS // 4):
                    if experts:
                        for n in range(2 * C1):
                            gelu1(b - 1, 2 * C1 * k + n)
                    if k < NS // 4 - 1:
                        for n in range(4 * k + 4, 4 * k + 8):
                            decays(n)

                layernorm(3, None, 0)
                route(1)
                act.wait_ge(gt_mm.sem, gt_mm.at(b, 1))
                f(gates_T[:], bank[MISC][0:E, :], ACT.Copy).then_inc(gt_out.sem, 1)
                assert step[0] == CHAIN_A_PER_BATCH, step[0]

            iteration(0, False)
            with act.Fori(1, B) as b:
                iteration(b, True)
            for n in range(E * C1):
                gelu1(B - 1, n)

        @block.vector
        def _(dve):
            v = nc.vector
            tt, ts, stt, cp = v.tensor_tensor, v.tensor_scalar, v.scalar_tensor_tensor, v.tensor_copy
            v.memset(eps_col[:], EPS)
            v.memset(xi[:], 0.0)
            v.memset(k_pad[:], 0.0)
            dve.wait_ge(weights_in, 16 * n_weights)
            cp(ident_bf[:], ident[:])
            cp(mask_bf[:], w["mask"][:])
            cp(select[:], w["stack"][:].unsqueeze(2).to_broadcast([3 * BC, BC, P]))
            ts(silu_half[:], w["cT"][:], 0.5, None, ALU.mult).then_inc(setup_v, 1)
            dve.wait_ge(setup_v, 1)
            dve.wait_ge(setup_a, 1)
            stt(silu_c[:], silu_tanh[:], 1.0, silu_half[:], ALU.add, ALU.mult).then_inc(setup_v, 1)
            dve.wait_ge(setup_v, 2)
            cp(silu_wide[:], silu_c[:].unsqueeze(3).to_broadcast([P, 2, B, P])).then_inc(setup_v, 1)
            dve.wait_ge(setup_a, 2)
            ts(a_neg[:], a_exp[:], -1.0, None, ALU.mult).then_inc(setup_v, 1)
            dve.wait_ge(setup_p, 1)
            cp(mod[:].rearrange("p l j b -> p (l j b)"), bank[2][:, 0:12 * B]).then_inc(setup_v, 1)
            dve.wait_ge(setup_v, 5)
            for k in (1, 4):
                ts(mod[:, :, k, :], mod[:, :, k, :], 1.0, None, ALU.add).then_inc(setup_v, 1)
            done = 7
            for b in range(B):
                dve.wait_ge(setup_p, 2 + b)
                g_row = bank[3 + b % 2][:].rearrange("p (k d) -> p k d", k=4)
                if b:
                    dve.wait_ge(setup_v, done)
                ts(gate_two[:], g_row, 0.0, 2.0, ALU.is_ge, ALU.mult).then_inc(setup_v2, 1)
                dve.wait_ge(setup_v2, 3 * b + 1)
                ts(gate_sign[:], gate_two[:], -1.0, None, ALU.add).then_inc(setup_v2, 1)
                dve.wait_ge(setup_v2, 3 * b + 2)
                tt(gate_size[:], g_row, gate_sign[:], ALU.mult).then_inc(setup_v2, 1)
                dve.wait_ge(setup_v2, 3 * b + 3)
                stt(gate[:, b, :, :], gate_size[:], 0.25, gate_sign[:], ALU.max, ALU.mult).then_inc(setup_v, 1)
                done += 1
            assert done == SETUP_V
            dve.wait_ge(setup_v, SETUP_V)

            def add_expert(b, n):
                e, t = divmod(n, NT)
                if t == 0:
                    dve.wait_ge(out1_mm.sem, out1_mm.at(b, (e + 1) * NT))
                dve.wait_ge(out1_add.sem, out1_add.at(b, 1 if e == 0 else n - NT + 2))
                stt(expert_sum[:, t, :], bank[OUT1_BANK[e % 2]][:, t * P:(t + 1) * P], gates[1][:, t, e:e + 1],
                    expert_sum[:, t, :], ALU.mult, ALU.add).then_inc(out1_add.sem, 1)

            def finish(b):
                dve.wait_ge(out1_add.sem, out1_add.at(b, E * NT + 1))
                dve.wait_ge(x_sent.sem, x_sent.before(b))
                tt(expert_out[:], expert_sum[:], gate[:, bass.ds(b, 1), 3, :].to_broadcast([P, NT, P]), ALU.mult
                   ).then_inc(out1_gate.sem, 1)
                dve.wait_ge(out1_gate.sem, out1_gate.at(b, 1))
                tt(x_out[:], x_mid[:], expert_out[:], ALU.add).then_inc(x_final.sem, 1)

            def iteration(b, experts):
                step = [0]

                def mark(ins):
                    step[0] += 1
                    ins.then_inc(chain.sem, 1)

                def sync():
                    dve.wait_ge(chain.sem, chain.at(b, step[0]))

                def link(ins):
                    mark(ins)
                    sync()

                def layernorm(j, x):
                    for t in range(NT):
                        ins = v.bn_stats(stats[:, t, :], x[:, t, :])
                    mark(ins)
                    sync()
                    v.memset(newton[:], 0.0)
                    for t in range(NT):
                        ins = v.bn_aggr(meanvar[:, t, :], stats[:, t, :])
                    ins.then_inc(ln_var.sem, 1)
                    dve.wait_ge(ln_var.sem, ln_var.at(b, j + 1))
                    mark(ts(var_eps[:], meanvar[:, :, 1], EPS, None, ALU.add))
                    dve.wait_ge(ln_r0.sem, ln_r0.at(b, j + 1))
                    link(tt(newton[:], rstd0[:], rstd0[:], ALU.mult))
                    link(tt(newton2[:], newton[:], var_eps[:], ALU.mult))
                    link(ts(newton3[:], newton2[:], -0.5, 1.5, ALU.mult, ALU.add))
                    link(tt(rstd[:], rstd0[:], newton3[:], ALU.mult))
                    link(stt(shift[:], meanvar[:, :, 0], -1.0, rstd[:], ALU.mult, ALU.mult))
                    for t in range(NT):
                        ins = ts(xn[:, t, :], x[:, t, :], rstd[:, t:t + 1], shift[:, t:t + 1], ALU.mult, ALU.add)
                    ins.then_inc(ln_xn.sem, 1)

                def add_mixed(k, source, to, done):
                    g_row = gate[:, bass.ds(b, 1), k, :].to_broadcast([P, NT, P])
                    link(tt(mixed[:], source, g_row, ALU.mult))
                    tt(to[:], x[:], mixed[:], ALU.add).then_inc(done.sem, 1)

                def route(layer):
                    wide = [P, NT, E]
                    dve.wait_ge(log_mm.sem, log_mm.at(b, layer + 1))
                    order = w["order"][:].unsqueeze(1).to_broadcast(wide)
                    link(cp(logits[:], bank[MISC][:, 0:NT * E].rearrange("p (t e) -> p t e", e=E)))
                    for k, (pick, values) in enumerate(((pick1, logits), (pick2, r_b))):
                        link(v.reduce_max(top[:, k, :], values[:], AX_X))
                        link(tt(r_a[:], values[:], top[:, k, :].unsqueeze(2).to_broadcast(wide), ALU.is_equal))
                        link(tt(r_a[:], r_a[:], order, ALU.mult))
                        link(v.reduce_max(best[:, k, :], r_a[:], AX_X))
                        link(tt(pick[:], r_a[:], best[:, k, :].unsqueeze(2).to_broadcast(wide), ALU.is_equal))
                        if k == 0:
                            link(stt(r_b[:], pick[:], FAR, logits[:], ALU.mult, ALU.add))
                    tt(gap[:], top[:, 1, :], top[:, 0, :], ALU.subtract).then_inc(gap_in.sem, 1)
                    dve.wait_ge(gap_out.sem, gap_out.at(b, layer + 1))
                    link(ts(gap_one[:], gap_exp[:], 1.0, None, ALU.add))
                    link(v.reciprocal(share1[:], gap_one[:]))
                    link(tt(share2[:], share1[:], gap_exp[:], ALU.mult))
                    mark(tt(r_a[:], pick1[:], share1[:].unsqueeze(2).to_broadcast(wide), ALU.mult))
                    link(tt(r_b[:], pick2[:], share2[:].unsqueeze(2).to_broadcast(wide), ALU.mult))
                    if layer == 0:
                        link(tt(gates[0][:], r_a[:], r_b[:], ALU.add))
                        cp(gates_wide[:].rearrange("p t e f -> p (t e) f"),
                           gates[0][:].rearrange("p t e -> p (t e)").unsqueeze(2).to_broadcast([P, NT * E, F0])
                           ).then_inc(gates_ok.sem, 1)
                    else:
                        tt(gates[1][:], r_a[:], r_b[:], ALU.add).then_inc(gates_ok.sem, 1)

                dve.wait_ge(x_loaded.sem, x_loaded.at(b, 16))
                cp(x[:], x_in[:]).then_inc(x_taken.sem, 1)
                dve.wait_ge(x_taken.sem, x_taken.at(b, 1))

                layernorm(0, x)
                for g in range(G):
                    dve.wait_ge(q_mm.sem, q_mm.at(b, G + g + 1))
                    for j in range(HG):
                        ins = cp(k_pad[j * L:(j + 1) * L, g, j, :], bank[2 + g][j * L:(j + 1) * L, :])
                    ins.then_inc(k_out.sem, 1)
                dve.wait_ge(v_mm.sem, v_mm.at(b, 1))
                cp(v_lat[:].rearrange("p t m -> p (t m)"), bank[OUT_BANK][:, 0:NT * G * L]).then_inc(v_out.sem, 1)

                def row_maximum(n):
                    i = n // 2 % NT
                    dve.wait_ge(s_mm.sem, s_mm.at(b, n + 1))
                    if n >= 2:
                        dve.wait_ge(s_exp.sem, s_exp.at(b, n - 1))
                    for jj in range(2):
                        ins = v.reduce_max(row_neg[:, n % 2, jj:jj + 1], bank[2 * (n % 2) + jj][:, 0:(i + 1) * P], AX_X)
                    link(ins)
                    ts(row_max[:, n % 2, :], row_neg[:, n % 2, :], -1.0, None, ALU.mult).then_inc(s_max.sem, 1)

                def take_transposed(n):
                    i, pair = n // 2 % NT, n % 2
                    for jj in range(2):
                        dve.wait_ge(p_T.sem, p_T.at(b, 2 * n + jj + 1))
                        if n == UNITS // 2 and jj == 0:
                            dve.wait_ge(y_mm.sem, y_mm.at(b, 1))
                        cp(probs_T[:, 2 * pair + jj, 0:i + 1, i * P:(i + 1) * P],
                           bank[4 + jj][:, 0:(i + 1) * P].rearrange("p (k q) -> p k q", q=P)).then_inc(p_out.sem, 1)

                def widen(g):
                    dve.wait_ge(s_exp.sem, s_exp.at(b, (g + 1) * 2 * NT))
                    link(v.reciprocal(row_inv[:], row_sum[:, g, :, :]))
                    cp(inv_wide[:].rearrange("p t h l -> p (t h) l"),
                       row_inv[:].rearrange("p t h -> p (t h)").unsqueeze(2).to_broadcast([P, NT * HG, L])
                       ).then_inc(inv_w.sem, 1)

                def normalise(g):
                    dve.wait_ge(inv_out.sem, inv_out.at(b, g + 1))
                    dve.wait_ge(y_mm.sem, y_mm.at(b, g + 1))
                    tt(y_T[:, g, :], bank[OUT_BANK][:], inv_T[:], ALU.mult).then_inc(y_out.sem, 1)

                row_maximum(0)
                for n in range(UNITS):
                    if n + 1 < UNITS:
                        row_maximum(n + 1)
                    if n == UNITS // 2:
                        widen(0)
                    if n == UNITS // 2 + 2:
                        normalise(0)
                    take_transposed(n)
                widen(1)
                normalise(1)
                dve.wait_ge(attn_mm.sem, attn_mm.at(b, 1))
                add_mixed(0, bank[MISC][:].rearrange("p (t d) -> p t d", d=P), x, attn_add)
                dve.wait_ge(attn_add.sem, attn_add.at(b, 1))

                layernorm(1, x)
                route(0)
                for c in range(C0):
                    dve.wait_ge(hid0_act.sem, hid0_act.at(b, c + 1))
                    dve.wait_ge(gT_mm.sem, gT_mm.at(b, c + 1))
                    tt(gated[:, c, :], hidden[:, c, :], bank[c % 2][:], ALU.mult).then_inc(hid0_gate.sem, 1)
                dve.wait_ge(out0_mm.sem, out0_mm.at(b, 1))
                add_mixed(1, bank[OUT_BANK][:].rearrange("p (t d) -> p t d", d=P), x, out0_add)
                dve.wait_ge(out0_add.sem, out0_add.at(b, 1))

                layernorm(2, x)
                for c in range(DH):
                    dve.wait_ge(in_out.sem, in_out.at(b, c + 1))
                    link(ts(conv[0][:, c, :], xi[:, c, 0:T], w["conv_w"][:, c, 0:1], w["conv_b"][:, c:c + 1],
                            ALU.mult, ALU.add))
                    for k in range(1, KC):
                        ins = stt(conv[k % 2][:, c, :], xi[:, c, k:k + T], w["conv_w"][:, c, k:k + 1],
                                  conv[(k - 1) % 2][:, c, :], ALU.mult, ALU.add)
                        if k < KC - 1:
                            link(ins)
                    ins.then_inc(conv_ok.sem, 1)
                for c in range(DH):
                    dve.wait_ge(conv_ok.sem, conv_ok.at(b, c + 1))
                    link(ts(conv[0][:, c, :], conv[1][:, c, :], 0.5, None, ALU.mult))
                    dve.wait_ge(tanh_ok.sem, tanh_ok.at(b, c + 1))
                    stt(xc[:, c, :], tanh_c[:, c, :], 1.0, conv[0][:, c, :], ALU.add, ALU.mult).then_inc(xc_ok.sem, 1)
                dve.wait_ge(xc_ok.sem, xc_ok.at(b, DH))
                for c in range(DH):
                    link(ts(conv[0][:, c, :], res[:, c, :], 0.5, None, ALU.mult))
                    dve.wait_ge(tanh_ok.sem, tanh_ok.at(b, DH + c + 1))
                    mark(stt(res_gate[:, c, :], tanh_c[:, c, :], 1.0, conv[0][:, c, :], ALU.add, ALU.mult))
                dve.wait_ge(pr_out.sem, pr_out.at(b, 1))
                link(cp(split[:], proj[0:3 * BC, :]))
                for lo, hi in ((L, 2 * L), (2 * L, 3 * L)):
                    link(tt(part[lo:hi, :], proj[lo:hi, :], split[lo:hi, :], ALU.subtract))
                    link(cp(split[lo:hi, :], part[lo:hi, :]))
                lo = 2 * L
                link(tt(part2[lo:lo + L, :], part[lo:lo + L, :], split[lo:lo + L, :], ALU.subtract))
                cp(split[lo:lo + L, :], part2[lo:lo + L, :]).then_inc(split_ok.sem, 1)
                for c in range(DH):
                    dve.wait_ge(dt_mm.sem, dt_mm.at(b, c + 1))
                    ts(dt_in[:, c, :], bank[HID0_BANK[c]][:], w["dt_b"][:, c:c + 1], None, ALU.add).then_inc(dt_z.sem, 1)
                for c in range(DH):
                    dve.wait_ge(dt_z.sem, dt_z.at(b, c + 1))
                    dve.wait_ge(dt_l.sem, dt_l.at(b, c + 1))
                    stt(delta[:, c, :], dt_in[:, c, :], 0.0, dt_log[:, c, :], ALU.max, ALU.add).then_inc(delta_ok.sem, 1)
                    dve.wait_ge(delta_ok.sem, delta_ok.at(b, c + 1))
                    tt(u[:, c, :], delta[:, c, :], xc[:, c, :], ALU.mult).then_inc(u_ok.sem, 1)
                dve.wait_ge(u_ok.sem, u_ok.at(b, DH))

                def inject_state(n):
                    dve.wait_ge(b_mm.sem, b_mm.at(b, n + 1))
                    tt(inject[:, n % 2, :, :], u[:], bank[BC_BANK[0]][:].unsqueeze(1).to_broadcast([P, DH, T]), ALU.mult
                       ).then_inc(inj_ok.sem, 1)

                inject_state(0)
                for n in range(NS):
                    if n + 1 < NS:
                        inject_state(n + 1)
                    for c in range(DH):
                        dve.wait_ge(dec_ok.sem, dec_ok.at(b, DH * n + c + 1))
                        if c == 0:
                            dve.wait_ge(inj_ok.sem, inj_ok.at(b, n + 1))
                        v.tensor_tensor_scan(state[:, n % 2, c, :], decay[:, n % 4, c, :], inject[:, n % 2, c, :], 0.0,
                                             ALU.mult, ALU.add).then_inc(st_ok.sem, 1)
                    if experts and n >= 3:
                        for k in range(4 * (n - 3 >= 0 and (n - 3) % 4 < 2)):
                            add_expert(b - 1, 8 * ((n - 3) // 4) + 4 * ((n - 3) % 4) + k)
                    dve.wait_ge(c_mm.sem, c_mm.at(b, n + 1))
                    dve.wait_ge(st_ok.sem, st_ok.at(b, DH * (n + 1)))
                    if n >= 2:
                        dve.wait_ge(acc_ok.sem, acc_ok.at(b, max(1, n - 2)))
                    tt(read[:, n % 2, :, :], state[:, n % 2, :, :],
                       bank[BC_BANK[1]][:].unsqueeze(1).to_broadcast([P, DH, T]), ALU.mult).then_inc(rd_ok.sem, 1)
                if experts:
                    for n in range(E * NT - 4, E * NT):
                        add_expert(b - 1, n)
                    finish(b - 1)
                dve.wait_ge(acc_ok.sem, acc_ok.at(b, NS - 1))
                for c in range(DH):
                    link(stt(y_skip[:, c, :], xc[:, c, :], w["d_skip"][:, c:c + 1], state_sum[:, c, :],
                             ALU.mult, ALU.add))
                    tt(z[:, c, :], y_skip[:, c, :], res_gate[:, c, :], ALU.mult).then_inc(z_ok.sem, 1)
                dve.wait_ge(mix_mm.sem, mix_mm.at(b, 1))
                link(tt(mixer_out[:], bank[OUT_BANK][:].rearrange("p (t d) -> p t d", d=P),
                        w["out_b"][:].unsqueeze(1).to_broadcast([P, NT, P]), ALU.add))
                add_mixed(2, mixer_out[:], x_mid, mix_add)
                dve.wait_ge(mix_add.sem, mix_add.at(b, 1))

                layernorm(3, x_mid)
                route(1)
                dve.wait_ge(b2_mm.sem, b2_mm.at(b, 1))
                cp(expert_sum[:].rearrange("p t d -> p (t d)"), bank[OUT_BANK][:]).then_inc(out1_add.sem, 1)
                assert step[0] == CHAIN_PER_BATCH, step[0]

            iteration(0, False)
            with dve.Fori(1, B) as b:
                iteration(b, True)
            for n in range(E * NT):
                add_expert(B - 1, n)
            finish(B - 1)


CHAIN_PER_BATCH = 105
CHAIN_A_PER_BATCH = 8
SETUP_V = 15
SETUP_A = 4


def _laid_out(a):
    c = lambda v: np.ascontiguousarray(v)
    g = {k: np.asarray(v) for k, v in a.items()}
    chunks = lambda v, n: c(v.reshape(n, P, -1).transpose(1, 0, 2))
    o = {"x": g["L0_attn_x"]}
    o["wqT"] = c(g["L0_attn_wq"].reshape(P, H, P).transpose(2, 1, 0))
    o["wk_upT"] = c(g["L0_attn_wk_up"].T)
    o["wv_upT"] = c(g["L0_attn_wv_up"].T)
    o["wk4"] = c(np.repeat(g["L0_attn_wk_down"].reshape(P, G, 1, L), HG, axis=2).reshape(P, G, HG * L))
    o["wv_down"] = g["L0_attn_wv_down"]
    o["wo"] = chunks(g["L0_attn_wo"], H)
    o["wg0"] = c(g["L0_ffn_w_gate"].T)
    o["wfcT"] = c(g["L0_ffn_w_fc"].reshape(E * F0, P).T)
    o["wprojT"] = chunks(g["L0_ffn_w_proj"].transpose(0, 2, 1).reshape(E * F0, P), C0)
    o["cT"] = c(np.stack([g["L0_c"].T, g["L1_c"].T], axis=1))
    o["wmod"] = c(np.stack([g["L0_wmod"], g["L1_wmod"]], axis=1))
    o["in_w"] = g["L1_attn_in_proj_w"]
    o["in_b"] = c(g["L1_attn_in_proj_b"].reshape(2 * DH, P).T)
    o["conv_w"] = c(g["L1_attn_conv_w"].reshape(KC, DH, P).transpose(2, 1, 0))
    o["conv_b"] = c(g["L1_attn_conv_b"].reshape(DH, P).T)
    order = np.concatenate([np.arange(NS, 3 * NS)] * 3 + [np.arange(NS)])
    o["x_proj_w"] = chunks(g["L1_attn_x_proj_w"][:, order], DH)
    o["x_proj_b"] = c(g["L1_attn_x_proj_b"][order].reshape(PR, 1))
    dt_w = np.zeros((PR, DI), np.float32)
    dt_w[3 * BC:] = g["L1_attn_dt_proj_w"]
    o["dt_w"] = dt_w
    o["dt_b"] = c(g["L1_attn_dt_proj_b"].reshape(DH, P).T)
    o["a_log"] = c(g["L1_attn_A_log"].reshape(DH, P, NS).transpose(1, 0, 2))
    o["d_skip"] = c(g["L1_attn_D_skip"].reshape(DH, P).T)
    o["out_w"] = chunks(g["L1_attn_out_proj_w"], DH)
    o["out_b"] = c(np.broadcast_to(g["L1_attn_out_proj_b"], (P, P)))
    o["wg1"] = g["L1_ffn_gate_w"]
    o["w1"] = c(g["L1_ffn_w1"].transpose(1, 0, 2))
    o["b1"] = c(g["L1_ffn_b1"].reshape(E * C1, P).T)
    o["w2"] = chunks(g["L1_ffn_w2"].reshape(E * F1, P), E * C1)
    o["b2"] = g["L1_ffn_b2"]
    o["ident"] = np.eye(P, dtype=np.float32)
    o["mask"] = np.triu(np.full((P, P), FAR, np.float32), 1)
    o["stack"] = np.tile(np.eye(BC, dtype=np.float32), (3, 1))
    o["order"] = c(np.broadcast_to(np.arange(E, 0, -1, dtype=np.float32), (P, E)))
    return o


def kernel(**inputs):
    import concourse.bacc as bacc
    from concourse.bass_utils import run_bass_kernel_spmd

    nc = bacc.Bacc("TRN2", target_bir_lowering=False, num_devices=1)
    arrays, io = {}, {}
    for name, a in _laid_out(inputs).items():
        a = np.ascontiguousarray(a)
        arrays[f"in_{name}_dram"] = a
        io[name] = nc.dram_tensor(f"in_{name}_dram", a.shape, mybir.dt.from_np(a.dtype), kind="ExternalInput").ap()
    out = nc.dram_tensor("out_0_dram", (B, T, P), F32, kind="ExternalOutput").ap()
    nc.disable_value_cache = True
    build(nc, io, out)
    r = run_bass_kernel_spmd(nc, [arrays], core_ids=[0])
    return r.results[0]["out_0_dram"]
```

```python
from contextlib import ExitStack

import numpy as np

import concourse.bass as bass
from concourse import mybir

F32 = mybir.dt.float32
BF16 = mybir.dt.bfloat16
I32 = mybir.dt.int32
ALU = mybir.AluOpType
ACT = mybir.ActivationFunctionType
AX_X = mybir.AxisListType.X

P = 128
B = 8
T = 512
NT = T // P
H = 8
G = 2
HG = H // G
L = 32
E = 8
F0 = 64
C0 = E * F0 // P
F1 = 512
C1 = F1 // P
DI = 256
DH = DI // P
NS = 16
KC = 4
BC = 2 * NS
PR = 3 * BC + NS
EPS = 1e-5
SCALE = float(P) ** -0.5
ROOT_GUESS = float(0x5F3759DF)
FAR = -3.0e38


class Signal:

    def __init__(self, sem, per_batch, primed):
        self.sem, self.per_batch, self.primed = sem, per_batch, primed

    def at(self, b, n):
        return b * self.per_batch + n + self.primed

    def before(self, b):
        assert self.primed
        return b * self.per_batch + self.primed


def build(nc, io, out):
    ctx = ExitStack()
    with ctx:
        def sb(name, shape, dt=F32):
            return ctx.enter_context(nc.sbuf_tensor(name, shape, dt))

        def sem(name):
            return ctx.enter_context(nc.semaphore(name))

        def signal(name, per_batch, primed=0):
            return Signal(sem(name), per_batch, primed)

        probs_T = sb("probs_T", [P, HG, NT, T])
        setup_space = probs_T[:].rearrange("p h k q -> p (h k q)")
        w = {name: sb("w_" + name, list(ap.shape)) for name, ap in io.items()
             if name not in ("x", "wqT", "wo", "wmod")}
        w["wqT"] = setup_space[:, 0:H * P].rearrange("p (h d) -> p h d", h=H)
        w["wo"] = setup_space[:, H * P:2 * H * P].rearrange("p (h d) -> p h d", h=H)
        w["wmod"] = setup_space[:, 2 * H * P:2 * H * P + 12 * P].rearrange("p (l d) -> p l d", l=2)
        pick = setup_space[0:B, 4 * H * P:4 * H * P + B * P].rearrange("p (b d) -> p b d", b=B)
        ident = w["ident"]

        ident_bf = sb("ident_bf", [P, P], BF16)
        mask_bf = sb("mask_bf", [P, P], BF16)
        select = sb("select", [3 * BC, BC, P], BF16)
        silu_c = sb("silu_c", [P, 2, B])
        silu_half = sb("silu_half", [P, 2, B])
        silu_tanh = sb("silu_tanh", [P, 2, B])
        mod = sb("mod", [P, 2, 6, B])
        gate = sb("gate", [P, B, 4, P])
        gate_sign, gate_size, gate_two, gate_rows = (
            setup_space[0:B, k * T:(k + 1) * T].rearrange("p (k d) -> p k d", k=4) for k in (12, 13, 14, 15))
        w_qk = sb("w_qk", [P, G, HG * L])
        w_vo = sb("w_vo", [P, G, P])
        a_neg = sb("a_neg", [P, DH, NS])
        a_exp = sb("a_exp", [P, DH, NS])

        x_in = sb("x_in", [P, NT, P])
        x = sb("x", [P, NT, P])
        x_out = sb("x_out", [P, NT, P])
        mixed = sb("mixed", [P, NT, P])
        x_mid = sb("x_mid", [P, NT, P])
        expert_out = sb("expert_out", [P, NT, P])
        mixer_out = sb("mixer_out", [P, NT, P])
        stats = sb("stats", [P, NT, 6])
        meanvar = sb("meanvar", [P, NT, 2])
        var_eps = sb("var_eps", [P, NT])
        newton = sb("newton", [P, NT])
        newton2 = sb("newton2", [P, NT])
        rstd = sb("rstd", [P, NT])
        shift = sb("shift", [P, NT])
        xn = sb("xn", [P, NT, P])
        hT = [sb(f"hT{j}", [P, T]) for j in range(4)]

        hidden = sb("hidden", [P, 2 * C1, T])
        q_lat = sb("q_lat", [P, G, T])
        k_pad = sb("k_pad", [P, G, HG, T])
        v_lat = sb("v_lat", [P, NT, G * L])
        row_neg = sb("row_neg", [P, 4])
        probs = sb("probs", [P, 2, 2, T])
        probs_ring = probs[:].rearrange("p a b k -> p (a b) k")
        row_sum = sb("row_sum", [P, G, NT, HG])
        row_inv = sb("row_inv", [P, 2, HG])
        inv_wide = hidden[:, 4, 0:2 * P].rearrange("p (t h l) -> p t h l", t=2, h=HG)
        inv_T = hidden[:, 5, 0:2 * P]
        y_T = hidden[:, G:2 * G, :]

        logits = sb("logits", [P, NT, E])
        r_a = sb("r_a", [P, NT, E])
        r_b = sb("r_b", [P, NT, E])
        top = sb("top", [P, 2, NT])
        best = sb("best", [P, 2, NT])
        pick1 = sb("pick1", [P, NT, E])
        pick2 = sb("pick2", [P, NT, E])
        gap = sb("gap", [P, NT])
        gap_exp = sb("gap_exp", [P, NT])
        gap_one = sb("gap_one", [P, NT])
        share1 = sb("share1", [P, NT])
        share2 = sb("share2", [P, NT])
        gates = [sb(f"gates{l}", [P, NT, E]) for l in range(2)]
        gates_wide = probs[:].rearrange("p a b (c f) -> p (a b) c f", f=F0)
        gates_T = sb("gates_T", [E, T])

        expert_sum = sb("expert_sum", [P, NT, P])

        xi = sb("xi", [P, DH, T + KC - 1])
        mix_space = probs_T[:].rearrange("p h k q -> p (h k q)")

        def within(first, *shape):
            n = int(np.prod(shape))
            flat = mix_space[:, first * T:(first + n) * T]
            if len(shape) == 1:
                return flat.rearrange("p (a t) -> p a t", a=shape[0])
            return flat.rearrange("p (a c t) -> p a c t", a=shape[0], c=shape[1])

        hid0 = within(8, C0)
        gated = within(12, C0)
        decay = within(0, 4, DH)
        inject = within(8, 2, DH)
        state = within(12, 2, DH)
        b_wide = hT[2]
        read = probs
        conv = [within(0, DH), within(DH, DH)]
        part = mix_space[0:3 * BC, 14 * T:15 * T]
        part2 = mix_space[0:3 * BC, 15 * T:16 * T]
        dt_exp, dt_abs, dt_log = conv[0], conv[1], within(8, DH)
        xc = sb("xc", [P, DH, T])
        res_gate = sb("res_gate", [P, DH, T])
        proj = sb("proj", [PR, T])
        split = sb("split", [3 * BC, T], BF16)
        dt_in = sb("dt_in", [P, DH, T])
        delta = sb("delta", [P, DH, T])
        u = sb("u", [P, DH, T])
        state_sum, y_skip, z = dt_in, delta, u

        bank = [ctx.enter_context(nc.psum_tensor(f"bank{i}", [P, T], F32)) for i in range(8)]
        BC_BANK, HID0_BANK, GATE_BANK, OUT_BANK, MISC = (0, 1), (4, 5), (0, 6), 6, 7
        PRE_BANK = 5
        ATTN_BANK = (0, MISC)
        EARLY_E = E // 2 - 2
        EARLY = (E // 2 - 1) * C1 + C1 // 2
        OUT1_BANK = (1,) * EARLY_E + ((6, 7) * E)[:E - EARLY_E]

        def hid1_bank(n):
            return bank[2 + n % 2] if n < EARLY else bank[2 + (n - EARLY) % 3]

        weights_in, experts_in = sem("weights_in"), sem("experts_in")
        setup_v, setup_a, setup_p, setup_gate = sem("setup_v"), sem("setup_a"), sem("setup_p"), sem("setup_gate")
        x_loaded = signal("x_loaded", 16)
        x_stored = signal("x_stored", 16)
        x_sent = signal("x_sent", 1, primed=1)
        x_taken = signal("x_taken", 1, primed=1)
        x_final = signal("x_final", 1)
        chain = signal("chain", CHAIN["main"])
        chain_pre = signal("chain_pre", NORM_STEPS - 1)
        chain_tail = signal("chain_tail", CHAIN["tail"])
        chain_norm = signal("chain_norm", NORM_STEPS - 1)
        chain_head = signal("chain_head", CHAIN["head"])
        chain_a = signal("chain_a", CHAIN["act main"])
        ln_xn, ln_T, h_ready = (
            (signal(name + "_first", 1), signal(name + "_later", 3))
            for name in ("ln_xn", "ln_T", "h_ready"))

        q_mm = signal("q_mm", 2 * G)
        q_out = signal("q_out", G)
        k_out = signal("k_out", G)
        v_mm = signal("v_mm", 1)
        v_out = signal("v_out", 1)
        UNITS = G * NT * HG
        s_mm = signal("s_mm", UNITS)
        s_max = signal("s_max", UNITS)
        s_exp = signal("s_exp", UNITS)
        p_T = signal("p_T", UNITS)
        BY_ACT = [n for n in range(UNITS) if n % 2 or n < ALL_BY_ACT]
        BY_DVE = [n for n in range(UNITS) if n not in BY_ACT]
        p_out_v = signal("p_out_v", len(BY_DVE))
        p_out_a = signal("p_out_a", len(BY_ACT))
        inv_w = signal("inv_w", 2 * G)
        y_mm = signal("y_mm", 2 * G)
        inv_out = signal("inv_out", 2 * G)
        y_out = signal("y_out", 2 * G)
        attn_mm = signal("attn_mm", 2)
        attn_add = signal("attn_add", 2)

        log_mm = signal("log_mm", 2)
        gap_in = signal("gap_in", 2)
        gap_out = signal("gap_out", 2)
        gates_ok = signal("gates_ok", 2)
        hid0_mm = signal("hid0_mm", C0)
        hid0_act = signal("hid0_act", C0)
        gT_mm = signal("gT_mm", C0)
        hid0_gate = signal("hid0_gate", C0)
        out0_mm = signal("out0_mm", 1)
        out0_add = signal("out0_add", 1)

        in_mm = signal("in_mm", 2 * DH)
        in_out = signal("in_out", 2 * DH)
        taps = signal("taps", (KC - 1) * DH)
        conv_ok = signal("conv_ok", DH)
        xc_ok = signal("xc_ok", DH)
        pr_mm = signal("pr_mm", 1)
        pr_out = signal("pr_out", 1)
        split_ok = signal("split_ok", 1)
        dt_mm = signal("dt_mm", DH)
        dt_z = signal("dt_z", DH)
        dt_l = signal("dt_l", DH)
        delta_ok = signal("delta_ok", DH)
        u_ok = signal("u_ok", DH)
        dec_ok = signal("dec_ok", NS * DH)
        b_mm = signal("b_mm", NS)
        c_mm = signal("c_mm", NS)
        inj_v = signal("inj_v", NS - NS // 3)
        b_out = signal("b_out", NS // 3)
        inj_p = signal("inj_p", NS // 3)
        st_ok = signal("st_ok", NS * DH)
        rd_ok = signal("rd_ok", NS)
        acc_ok = signal("acc_ok", NS - 1)
        z_ok = signal("z_ok", DH)
        mix_mm = signal("mix_mm", 1)
        mix_add = signal("mix_add", 1)

        gt_mm = signal("gt_mm", 1)
        gt_out = signal("gt_out", 1)
        b2_mm = signal("b2_mm", 1)
        hid1_mm = signal("hid1_mm", E * C1)
        hid1_act = signal("hid1_act", E * C1)
        out1_mm = signal("out1_mm", E * NT)
        out1_add = signal("out1_add", E * NT + 1)
        out1_gate = signal("out1_gate", 1)

        def taken(eng, b, n):
            by, units = (p_out_a, BY_ACT) if n in BY_ACT else (p_out_v, BY_DVE)
            eng.wait_ge(by.sem, by.at(b, units.index(n) + 1))

        def by_pool(n):
            return n % 3 == 2

        def b_read(eng, b, n):
            if by_pool(n):
                eng.wait_ge(b_out.sem, b_out.at(b, n // 3 + 1))
            else:
                injected(eng, b, n)

        def injected(eng, b, n):
            if by_pool(n):
                eng.wait_ge(inj_p.sem, inj_p.at(b, n // 3 + 1))
            else:
                eng.wait_ge(inj_v.sem, inj_v.at(b, n + 1 - (n + 1) // 3))

        def transposed(n):
            i, j = n // HG % NT, n % HG
            return (probs_T[:, j, 0:i + 1, i * P:(i + 1) * P],
                    bank[4 + n % 2][:, 0:(i + 1) * P].rearrange("p (k q) -> p k q", q=P))

        def of(pair, j):
            return pair[j > 0].sem

        def nth(pair, b, j):
            return of(pair, j), pair[j > 0].at(b, max(j, 1))

        def linker(eng, sig, b):
            count = [0]

            def mark(ins):
                count[0] += 1
                ins.then_inc(sig.sem, 1)

            def link(ins):
                mark(ins)
                eng.wait_ge(sig.sem, sig.at(b, count[0]))

            def check():
                assert count[0] == sig.per_batch, (sig.sem, count[0])

            return mark, link, check

        n_weights = len(w) - len(LATE)
        block = ctx.enter_context(nc.Block())

        @block.sync
        def _(sp):
            for name, tile in w.items():
                if name not in LATE:
                    sp.dma_start(tile[:], io[name]).then_inc(weights_in, 16)
            for name in LATE:
                sp.dma_start(w[name][:], io[name]).then_inc(experts_in, 16)
            for s in (x_sent, x_taken):
                sp.sem_inc(s.sem, 1)

        @block.gpsimd
        def _(pool):
            x_rows = io["x"].rearrange("b (t p) d -> b p t d", p=P)
            out_rows = out.rearrange("b (t p) d -> b p t d", p=P)

            def load(b):
                pool.wait_ge(x_taken.sem, x_taken.before(b))
                pool.dma_start(x_in[:], x_rows[bass.ds(b, 1), :, :, :].rearrange("a p t d -> p (a t) d")
                               ).then_inc(x_loaded.sem, 16)

            def store(b):
                pool.wait_ge(x_final.sem, x_final.at(b, 1))
                pool.dma_start(out_rows[bass.ds(b, 1), :, :, :].rearrange("a p t d -> p (a t) d"), x_out[:]
                               ).then_inc(x_stored.sem, 16)
                pool.wait_ge(x_stored.sem, x_stored.at(b, 16))
                pool.sem_inc(x_sent.sem, 1)

            def sum_states(b):
                for n in range(1, NS):
                    if by_pool(n + 1):
                        if n == 1:
                            pool.wait_ge(u_ok.sem, u_ok.at(b, DH))
                        pool.wait_ge(st_ok.sem, st_ok.at(b, DH * n))
                        pool.wait_ge(b_out.sem, b_out.at(b, (n + 1) // 3 + 1))
                        nc.gpsimd.tensor_tensor(inject[:, (n + 1) % 2, :, :], u[:],
                                                b_wide[:].unsqueeze(1).to_broadcast([P, DH, T]), ALU.mult
                                                ).then_inc(inj_p.sem, 1)
                    pool.wait_ge(rd_ok.sem, rd_ok.at(b, n + 1))
                    if n == 1:
                        ins = nc.gpsimd.tensor_tensor(state_sum[:], read[:, 0, :, :], read[:, 1, :, :], ALU.add)
                    else:
                        pool.wait_ge(acc_ok.sem, acc_ok.at(b, n - 1))
                        ins = nc.gpsimd.tensor_tensor(state_sum[:], state_sum[:], read[:, n % 2, :, :], ALU.add)
                    ins.then_inc(acc_ok.sem, 1)

            load(0)
            load(1)
            sum_states(0)
            with pool.Fori(1, B - 1) as b:
                load(b + 1)
                sum_states(b)
                store(b - 1)
            sum_states(B - 1)
            store(B - 2)
            store(B - 1)

        @block.tensor
        def _(pe):
            mm, tr = nc.tensor.matmul, nc.tensor.transpose

            pe.wait_ge(weights_in, 16 * n_weights)
            for h in range(H):
                ins = mm(bank[0][:, h * L:(h + 1) * L], w["wqT"][:, h, :], w["wk_upT"][:], start=True, stop=True)
            for h in range(H):
                g, j = divmod(h, HG)
                ins = mm(bank[1][j * L:(j + 1) * L, g * P:(g + 1) * P], w["wv_upT"][:], w["wo"][:, h, :],
                         start=True, stop=True)
            pe.wait_ge(setup_v, 3)
            for l in range(2):
                for j in range(6):
                    ins = mm(bank[2][:, (l * 6 + j) * B:(l * 6 + j + 1) * B], w["wmod"][:, l, j * P:(j + 1) * P],
                             silu_c[:, l, :], start=True, stop=True)
            ins.then_inc(setup_p, 1)
            for k in range(4):
                l, j = k // 2, 2 if k % 2 == 0 else 5
                ins = mm(bank[3][0:B, k * P:(k + 1) * P], silu_c[:, l, :], w["wmod"][:, l, j * P:(j + 1) * P],
                         start=True, stop=True)
            ins.then_inc(setup_p, 1)
            pe.wait_ge(setup_v, 7)
            pe.wait_ge(setup_a, 4)

            def layernorm(b, j, to, free=None):
                if free:
                    pe.wait_ge(*free)
                pe.wait_ge(*nth(ln_xn, b, j))
                for t in range(NT):
                    ins = tr(bank[to][:, t * P:(t + 1) * P], xn[:, t, :], ident[:])
                ins.then_inc(of(ln_T, j), 1)

            def h_wait(b, j):
                pe.wait_ge(*nth(h_ready, b, j))

            def router(b, layer, weight):
                for t in range(NT):
                    ins = mm(bank[MISC][:, t * E:(t + 1) * E], hT[2 * layer + 1][:, t * P:(t + 1) * P], weight[:],
                             start=True, stop=True)
                ins.then_inc(log_mm.sem, 1)

            def hid1(b, n):
                last = n - 2 if n < EARLY + 2 else n - 3
                if last >= 0:
                    pe.wait_ge(hid1_act.sem, hid1_act.at(b, last + 1))
                mm(hid1_bank(n)[:], w["w1"][:, n // C1, n % C1 * P:(n % C1 + 1) * P], hT[3][:],
                   start=True, stop=True).then_inc(hid1_mm.sem, 1)

            def out1(b, n):
                e, t = divmod(n, NT)
                if t == 0:
                    pe.wait_ge(hid1_act.sem, hid1_act.at(b, (e + 1) * C1))
                    if 1 <= e < EARLY_E or e >= EARLY_E + 2:
                        last = e - 1 if e < EARLY_E else e - 2
                        pe.wait_ge(out1_add.sem, out1_add.at(b, (last + 1) * NT + 1))
                for c in range(C1):
                    ins = mm(bank[OUT1_BANK[e]][:, t * P:(t + 1) * P], hidden[:, (e * C1 + c) % (2 * C1), t * P:(t + 1) * P],
                             w["w2"][:, e * C1 + c, :], start=(c == 0), stop=(c == C1 - 1))
                ins.then_inc(out1_mm.sem, 1)

            def project(b, k):
                if k == 0:
                    h_wait(b, 0)
                elif k == 1:
                    pe.wait_ge(q_out.sem, q_out.at(b, 1))
                elif k == 2:
                    pe.wait_ge(q_out.sem, q_out.at(b, 2))
                else:
                    pe.wait_ge(k_out.sem, k_out.at(b, k - 2))
                to = bank[PRE_BANK]
                if k < 4:
                    mm(to[:], w_qk[:, k, :] if k < 2 else w["wk4"][:, k - 2, :], hT[0][:], start=True, stop=True
                       ).then_inc(q_mm.sem, 1)
                else:
                    for t in range(NT):
                        ins = mm(to[:, t * G * L:(t + 1) * G * L], hT[0][:, t * P:(t + 1) * P], w["wv_down"][:],
                                 start=True, stop=True)
                    ins.then_inc(v_mm.sem, 1)

            def expert_head(b, k):
                if k == 0:
                    layernorm(b, 3, MISC)
                elif k == 1:
                    h_wait(b, 3)
                    router(b, 1, w["wg1"])
                elif k == 2:
                    pe.wait_ge(gates_ok.sem, gates_ok.at(b, 2))
                    for t in range(NT):
                        ins = tr(bank[MISC][0:E, t * P:(t + 1) * P], gates[1][:, t, :], ident[:])
                    ins.then_inc(gt_mm.sem, 1)
                else:
                    pe.wait_ge(gt_out.sem, gt_out.at(b, 1))
                    for t in range(NT):
                        ins = mm(bank[MISC][:, t * P:(t + 1) * P], gates_T[:, t * P:(t + 1) * P], w["b2"][:],
                                 start=True, stop=True)
                    ins.then_inc(b2_mm.sem, 1)

            def mixer_out_mm(b):
                pe.wait_ge(z_ok.sem, z_ok.at(b, DH))
                for t in range(NT):
                    for c in range(DH):
                        ins = mm(bank[OUT_BANK][:, t * P:(t + 1) * P], z[:, c, t * P:(t + 1) * P], w["out_w"][:, c, :],
                                 start=(c == 0), stop=(c == DH - 1))
                ins.then_inc(mix_mm.sem, 1)

            def iteration(b, behind, ahead):
                def early(e, chunks=(), out=False):
                    if behind:
                        for c in chunks:
                            hid1(b - 1, e * C1 + c)
                        if out:
                            for t in range(NT):
                                out1(b - 1, e * NT + t)

                def scores(n):
                    g, i, j = n // (NT * HG), n // HG % NT, n % HG
                    if n < 2 and behind:
                        if n == 0:
                            b_read(pe, b - 1, NS - 1)
                        else:
                            pe.wait_ge(rd_ok.sem, rd_ok.at(b - 1, NS))
                    if n == 0:
                        pe.wait_ge(k_out.sem, k_out.at(b, G))
                        pe.wait_ge(v_out.sem, v_out.at(b, 1))
                    if n >= 4:
                        pe.wait_ge(s_exp.sem, s_exp.at(b, n - 3))
                    s = bank[n % 4]
                    mm(s[:, 0:(i + 1) * P], q_lat[:, g, i * P:(i + 1) * P], k_pad[:, g, j, 0:(i + 1) * P],
                       start=True, stop=False)
                    mm(s[:, i * P:(i + 1) * P], ident_bf[:], mask_bf[:], start=False, stop=True).then_inc(s_mm.sem, 1)

                def transposes(n):
                    i = n // HG % NT
                    pe.wait_ge(s_exp.sem, s_exp.at(b, n + 1))
                    if n >= 2:
                        taken(pe, b, n - 2)
                    for k in range(i + 1):
                        ins = tr(bank[4 + n % 2][:, k * P:(k + 1) * P], probs_ring[:, n % 4, k * P:(k + 1) * P], ident[:])
                    ins.then_inc(p_T.sem, 1)

                def values(half):
                    g, first = half // 2, half % 2 * 2
                    for n in range(8 * half + 4, 8 * half + 8):
                        taken(pe, b, n)
                    if half > 0:
                        pe.wait_ge(y_out.sem, y_out.at(b, half))
                    elif behind:
                        pe.wait_ge(mix_add.sem, mix_add.at(b - 1, 1))
                    for k in range(first + 2):
                        at = max(k, first)
                        for j in range(HG):
                            mm(bank[OUT_BANK][j * L:(j + 1) * L, (at - first) * P:2 * P], v_lat[:, k, g * L:(g + 1) * L],
                               probs_T[:, j, k, at * P:(first + 2) * P], start=(k == 0), stop=(k == first + 1),
                               skip_group_check=True)
                    pe.wait_ge(inv_w.sem, inv_w.at(b, half + 1))
                    for t in range(2):
                        ins = tr(bank[OUT_BANK][:, (2 + t) * P:(3 + t) * P],
                                 inv_wide[:, t, :, :].rearrange("p h l -> p (h l)"), ident[:])
                    ins.then_inc(y_mm.sem, 1)

                def attention_out(half):
                    pe.wait_ge(y_out.sem, y_out.at(b, G + half + 1))
                    for t in range(2 * half, 2 * half + 2):
                        for g in range(G):
                            ins = mm(bank[ATTN_BANK[half]][:, t * P:(t + 1) * P], y_T[:, g, t * P:(t + 1) * P],
                                     w_vo[:, g, :], start=(g == 0), stop=(g == G - 1))
                    ins.then_inc(attn_mm.sem, 1)

                for n in range(UNITS + LAG):
                    if n < UNITS:
                        scores(n)
                    if n >= LAG:
                        transposes(n - LAG)
                    if behind and n == 5:
                        mixer_out_mm(b - 1)
                    if behind and n in PE_HEAD:
                        expert_head(b - 1, PE_HEAD.index(n))
                    if n in (12, 20, 28):
                        values(n // 8 - 1)
                attention_out(0)
                values(3)
                if behind:
                    pe.wait_ge(out1_add.sem, out1_add.at(b - 1, 1))
                attention_out(1)
                early(0, range(C1))

                layernorm(b, 1, MISC, (attn_add.sem, attn_add.at(b, 2)))
                h_wait(b, 1)
                router(b, 0, w["wg0"])
                for c in range(C0):
                    if c >= 2:
                        pe.wait_ge(hid0_act.sem, hid0_act.at(b, c - 1))
                    mm(bank[HID0_BANK[c % 2]][:], w["wfcT"][:, c * P:(c + 1) * P], hT[1][:], start=True, stop=True
                       ).then_inc(hid0_mm.sem, 1)
                pe.wait_ge(gates_ok.sem, gates_ok.at(b, 1))
                for c in range(C0):
                    if c == 2:
                        early(1, (0, 1))
                    if c >= 2:
                        pe.wait_ge(hid0_gate.sem, hid0_gate.at(b, c - 1))
                    for t in range(NT):
                        wide = gates_wide[:, t, :, :].rearrange("p e f -> p (e f)")
                        ins = tr(bank[GATE_BANK[c % 2]][:, t * P:(t + 1) * P], wide[:, c * P:(c + 1) * P], ident[:])
                    ins.then_inc(gT_mm.sem, 1)
                pe.wait_ge(hid0_gate.sem, hid0_gate.at(b, C0))
                for t in range(NT):
                    for c in range(C0):
                        ins = mm(bank[OUT_BANK][:, t * P:(t + 1) * P], gated[:, c, t * P:(t + 1) * P],
                                 w["wprojT"][:, c, :], start=(c == 0), stop=(c == C0 - 1))
                ins.then_inc(out0_mm.sem, 1)
                early(1, (2, 3))
                early(0, out=True)
                early(2, (0, 1))

                layernorm(b, 2, MISC, (gates_ok.sem, gates_ok.at(b, 1)))
                h_wait(b, 2)
                for c in range(2 * DH):
                    if c >= 2:
                        pe.wait_ge(in_out.sem, in_out.at(b, c - 1))
                    mm(bank[HID0_BANK[c % 2]][:], w["in_w"][:, c * P:(c + 1) * P], hT[2][:], start=True, stop=True
                       ).then_inc(in_mm.sem, 1)
                early(1, out=True)
                for c in range(DH):
                    pe.wait_ge(xc_ok.sem, xc_ok.at(b, c + 1))
                    ins = mm(bank[MISC][0:PR, :], w["x_proj_w"][:, c, :], xc[:, c, :], start=(c == 0), stop=(c == DH - 1))
                ins.then_inc(pr_mm.sem, 1)
                early(2, (2, 3))
                pe.wait_ge(pr_out.sem, pr_out.at(b, 1))
                pe.wait_ge(in_out.sem, in_out.at(b, 2 * DH))
                for c in range(DH):
                    mm(bank[HID0_BANK[c]][:], w["dt_w"][:, c * P:(c + 1) * P], proj[:], start=True, stop=True
                       ).then_inc(dt_mm.sem, 1)
                early(3, (0, 1))
                pe.wait_ge(split_ok.sem, split_ok.at(b, 1))
                pe.wait_ge(dt_z.sem, dt_z.at(b, DH))

                def spread_b(n):
                    if n >= 1:
                        b_read(pe, b, n - 1)
                    mm(bank[BC_BANK[0]][:], select[:, n, :], split[:], start=True, stop=True).then_inc(b_mm.sem, 1)

                def expert_pieces(n):
                    if behind:
                        for m in range(*SCAN_HIDDEN.get(n, (0,))):
                            hid1(b - 1, m)
                        for m in range(*SCAN_OUTPUT.get(n, (0,))):
                            out1(b - 1, m)

                spread_b(0)
                early(2, out=True)
                spread_b(1)
                if behind:
                    pe.wait_ge(out1_add.sem, out1_add.at(b - 1, EARLY_E * NT + 1))
                for n in range(NS):
                    if n >= 1:
                        pe.wait_ge(rd_ok.sem, rd_ok.at(b, n))
                    mm(bank[BC_BANK[1]][:], select[:, NS + n, :], split[:], start=True, stop=True).then_inc(c_mm.sem, 1)
                    if n + 2 < NS:
                        spread_b(n + 2)
                    expert_pieces(n)
                    if ahead:
                        if n == 8:
                            layernorm(b + 1, 0, PRE_BANK)
                        elif 8 < n < 14:
                            project(b + 1, n - 9)

            layernorm(0, 0, PRE_BANK)
            for k in range(5):
                project(0, k)
            pe.wait_ge(setup_v, SETUP_V)
            for b in range(B):
                if b >= 2:
                    pe.wait_ge(setup_a, 4 + b - 1)
                mm(bank[3 + b % 2][:], pick[:, b, :], gate_rows[:].rearrange("p k d -> p (k d)"), start=True, stop=True
                   ).then_inc(setup_p, 1)
            pe.wait_ge(setup_a, SETUP_A)
            iteration(0, False, True)
            pe.wait_ge(experts_in, 16 * len(LATE))
            with pe.Fori(1, B - 1) as b:
                iteration(b, True, True)
            iteration(B - 1, True, False)
            mixer_out_mm(B - 1)
            expert_head(B - 1, 0)
            expert_head(B - 1, 1)
            for n in range(C1):
                hid1(B - 1, n)
            expert_head(B - 1, 2)
            for n in range(C1, C1 + 2):
                hid1(B - 1, n)
            expert_head(B - 1, 3)
            for n in range(C1 + 2, 2 * C1):
                hid1(B - 1, n)
            for e in range(E):
                for t in range(NT):
                    out1(B - 1, e * NT + t)
                for n in range((e + 2) * C1, min(e + 3, E) * C1):
                    hid1(B - 1, n)

        @block.scalar
        def _(act):
            f = nc.scalar.activation
            act.wait_ge(weights_in, 16 * n_weights)
            f(silu_tanh[:], w["cT"][:], ACT.Tanh, scale=0.5).then_inc(setup_a, 1)
            f(a_exp[:], w["a_log"][:], ACT.Exp).then_inc(setup_a, 1)
            act.wait_ge(setup_p, 1)
            f(w_qk[:].rearrange("p g m -> p (g m)"), bank[0][:, 0:H * L], ACT.Copy, scale=SCALE).then_inc(setup_a, 1)
            f(w_vo[:].rearrange("p g m -> p (g m)"), bank[1][:, 0:G * P], ACT.Copy).then_inc(setup_a, 1)
            act.wait_ge(setup_v, 7)

            def gelu1(b, n):
                act.wait_ge(hid1_mm.sem, hid1_mm.at(b, n + 1))
                if n >= 2 * C1 and n % C1 == 0:
                    act.wait_ge(out1_mm.sem, out1_mm.at(b, NT * (n // C1 - 1)))
                f(hidden[:, n % (2 * C1), :], hid1_bank(n)[:], ACT.Gelu, bias=w["b1"][:, n:n + 1]
                  ).then_inc(hid1_act.sem, 1)

            def ln_modulate(b, j, source):
                act.wait_ge(*nth(ln_T, b, j))
                l, k = j // 2, 3 * (j % 2)
                f(hT[j][:], bank[source][:], ACT.Identity, bias=mod[:, l, k, bass.ds(b, 1)],
                  scale=mod[:, l, k + 1, bass.ds(b, 1)]).then_inc(of(h_ready, j), 1)

            def route(b, layer):
                act.wait_ge(gap_in.sem, gap_in.at(b, layer + 1))
                f(gap_exp[:], gap[:], ACT.Exp).then_inc(gap_out.sem, 1)

            def take_queries(b, g):
                act.wait_ge(q_mm.sem, q_mm.at(b, g + 1))
                f(q_lat[:, g, :], bank[PRE_BANK][:], ACT.Copy).then_inc(q_out.sem, 1)

            def take_keys(b, g):
                act.wait_ge(q_mm.sem, q_mm.at(b, G + g + 1))
                for j in range(HG):
                    ins = f(k_pad[j * L:(j + 1) * L, g, j, :], bank[PRE_BANK][j * L:(j + 1) * L, :], ACT.Copy)
                ins.then_inc(k_out.sem, 1)

            def take_values(b):
                act.wait_ge(v_mm.sem, v_mm.at(b, 1))
                f(v_lat[:].rearrange("p t m -> p (t m)"), bank[PRE_BANK][:, 0:NT * G * L], ACT.Copy).then_inc(v_out.sem, 1)

            def expert_head(b, k):
                if k == 0:
                    ln_modulate(b, 3, MISC)
                elif k == 1:
                    route(b, 1)
                else:
                    act.wait_ge(gt_mm.sem, gt_mm.at(b, 1))
                    f(gates_T[:], bank[MISC][0:E, :], ACT.Copy).then_inc(gt_out.sem, 1)

            def iteration(b, behind, ahead):
                mark, _, check = linker(act, chain_a, b)

                def early(e, chunks):
                    for c in chunks:
                        if behind:
                            gelu1(b - 1, e * C1 + c)

                def take_transposed(n):
                    act.wait_ge(p_T.sem, p_T.at(b, n + 1))
                    if n >= UNITS // 2 and n % 8 == 1:
                        act.wait_ge(y_mm.sem, y_mm.at(b, n // 8 - 1))
                    to, source = transposed(n)
                    f(to, source, ACT.Copy).then_inc(p_out_a.sem, 1)

                def take_inverse(half):
                    act.wait_ge(y_mm.sem, y_mm.at(b, half + 1))
                    if half > 0:
                        act.wait_ge(y_out.sem, y_out.at(b, half))
                    f(inv_T[:], bank[OUT_BANK][:, 2 * P:4 * P], ACT.Copy).then_inc(inv_out.sem, 1)

                for n in range(UNITS):
                    g, i, j = n // (NT * HG), n // HG % NT, n % HG
                    if n - LAG in BY_ACT:
                        take_transposed(n - LAG)
                    act.wait_ge(s_max.sem, s_max.at(b, n + 1))
                    if behind and n in (0, 2):
                        act.wait_ge(acc_ok.sem, acc_ok.at(b - 1, NS - 2 + n // 2))
                    if n >= 4:
                        act.wait_ge(p_T.sem, p_T.at(b, n - 3))
                    f(probs_ring[:, n % 4, 0:(i + 1) * P], bank[n % 4][:, 0:(i + 1) * P], ACT.Exp,
                      bias=row_neg[:, n % 4:n % 4 + 1], accum_out=row_sum[:, g, i, j:j + 1]).then_inc(s_exp.sem, 1)
                    if behind and n in ACT_HEAD:
                        expert_head(b - 1, ACT_HEAD.index(n))
                    if n in (13, 21, 29):
                        take_inverse(n // 8 - 1)
                for n in range(UNITS - LAG, UNITS):
                    if n in BY_ACT:
                        take_transposed(n)
                take_inverse(3)

                early(0, range(C1))
                ln_modulate(b, 1, MISC)
                route(b, 0)
                for c in range(C0):
                    act.wait_ge(hid0_mm.sem, hid0_mm.at(b, c + 1))
                    f(hid0[:, c, :], bank[HID0_BANK[c % 2]][:], ACT.Gelu).then_inc(hid0_act.sem, 1)
                early(1, (0, 1, 2, 3))

                early(2, (0, 1))
                ln_modulate(b, 2, MISC)
                for c in range(2 * DH):
                    act.wait_ge(in_mm.sem, in_mm.at(b, c + 1))
                    to, func = (xi[:, c, KC - 1:], ACT.Identity) if c < DH else (res_gate[:, c - DH, :], ACT.Silu)
                    f(to, bank[HID0_BANK[c % 2]][:], func, bias=w["in_b"][:, c:c + 1]).then_inc(in_out.sem, 1)
                for c in range(DH):
                    act.wait_ge(conv_ok.sem, conv_ok.at(b, c + 1))
                    f(xc[:, c, :], conv[1][:, c, :], ACT.Silu).then_inc(xc_ok.sem, 1)
                act.wait_ge(pr_mm.sem, pr_mm.at(b, 1))
                f(proj[:], bank[MISC][0:PR, :], ACT.Identity, bias=w["x_proj_b"][:]).then_inc(pr_out.sem, 1)
                early(2, (2, 3))
                for c in range(DH):
                    act.wait_ge(dt_mm.sem, dt_mm.at(b, c + 1))
                    mark(f(dt_abs[:, c, :], bank[HID0_BANK[c]][:], ACT.Abs, bias=w["dt_b"][:, c:c + 1]))
                for c in range(DH):
                    act.wait_ge(chain_a.sem, chain_a.at(b, c + 1))
                    mark(f(dt_exp[:, c, :], dt_abs[:, c, :], ACT.Exp, scale=-1.0))
                for c in range(DH):
                    act.wait_ge(chain_a.sem, chain_a.at(b, DH + c + 1))
                    f(dt_log[:, c, :], dt_exp[:, c, :], ACT.Ln, bias=1.0).then_inc(dt_l.sem, 1)

                def decays(n):
                    for c in range(DH):
                        if n >= 4:
                            act.wait_ge(st_ok.sem, st_ok.at(b, (n - 4) * DH + c + 1))
                        f(decay[:, n % 4, c, :], delta[:, c, :], ACT.Exp, scale=a_neg[:, c, n:n + 1]
                          ).then_inc(dec_ok.sem, 1)

                act.wait_ge(delta_ok.sem, delta_ok.at(b, DH))
                def take_b(n):
                    act.wait_ge(b_mm.sem, b_mm.at(b, n + 1))
                    if n > 2:
                        act.wait_ge(inj_p.sem, inj_p.at(b, n // 3))
                    f(b_wide[:], bank[BC_BANK[0]][:], ACT.Copy).then_inc(b_out.sem, 1)

                for n in range(4):
                    decays(n)
                take_b(2)
                gelus = {0: range(EARLY - 2, 20), 1: range(20, 28), 2: range(28, E * C1)}
                for k in range(NS // 4 - 1):
                    if ahead and k == 2:
                        ln_modulate(b + 1, 0, PRE_BANK)
                    for m in gelus[k]:
                        if m == 24:
                            take_b(8)
                        if behind:
                            gelu1(b - 1, m)
                    for n in range(4 * k + 4, 4 * k + 8):
                        if n == 15:
                            take_b(14)
                        if ahead and 12 <= n < 14:
                            take_queries(b + 1, n - 12)
                        elif ahead and n >= 14:
                            take_keys(b + 1, n - 14)
                        if n in (7, 11):
                            take_b(n // 4 * 6 - 1)
                        decays(n)
                if ahead:
                    take_values(b + 1)
                check()

            ln_modulate(0, 0, PRE_BANK)
            for g in range(G):
                take_queries(0, g)
            for g in range(G):
                take_keys(0, g)
            take_values(0)
            for b in range(B):
                act.wait_ge(setup_p, 3 + b)
                f(gate[:, b, :, :], bank[3 + b % 2][:].rearrange("p (k d) -> p k d", k=4), ACT.Copy).then_inc(setup_a, 1)
            iteration(0, False, True)
            with act.Fori(1, B - 1) as b:
                iteration(b, True, True)
            iteration(B - 1, True, False)
            expert_head(B - 1, 0)
            for n in range(E * C1):
                if n in (2, 4):
                    expert_head(B - 1, n // 2)
                gelu1(B - 1, n)

        @block.vector
        def _(dve):
            v = nc.vector
            tt, ts, stt, cp = v.tensor_tensor, v.tensor_scalar, v.scalar_tensor_tensor, v.tensor_copy
            v.memset(xi[:], 0.0)
            v.memset(k_pad[:], 0.0)
            dve.wait_ge(weights_in, 16 * n_weights)
            cp(ident_bf[:], ident[:])
            cp(mask_bf[:], w["mask"][:])
            cp(select[:], w["stack"][:].unsqueeze(2).to_broadcast([3 * BC, BC, P]))
            ts(silu_half[:], w["cT"][:], 0.5, None, ALU.mult).then_inc(setup_v, 1)
            dve.wait_ge(setup_v, 1)
            dve.wait_ge(setup_a, 1)
            stt(silu_c[:], silu_tanh[:], 1.0, silu_half[:], ALU.add, ALU.mult).then_inc(setup_v, 1)
            dve.wait_ge(setup_v, 2)
            cp(pick[:], ident[0:B, 0:B].unsqueeze(2).to_broadcast([B, B, P])).then_inc(setup_v, 1)
            dve.wait_ge(setup_a, 2)
            ts(a_neg[:], a_exp[:], -1.0, None, ALU.mult).then_inc(setup_v, 1)
            dve.wait_ge(setup_p, 1)
            cp(mod[:].rearrange("p l j b -> p (l j b)"), bank[2][:, 0:12 * B]).then_inc(setup_v, 1)
            dve.wait_ge(setup_v, 5)
            for k in (1, 4):
                ts(mod[:, :, k, :], mod[:, :, k, :], 1.0, None, ALU.add).then_inc(setup_v, 1)
            dve.wait_ge(setup_p, 2)
            g_row = bank[3][0:B, :].rearrange("p (k d) -> p k d", k=4)
            ts(gate_two[:], g_row, 0.0, 2.0, ALU.is_ge, ALU.mult).then_inc(setup_gate, 1)
            dve.wait_ge(setup_gate, 1)
            ts(gate_sign[:], gate_two[:], -1.0, None, ALU.add).then_inc(setup_gate, 1)
            dve.wait_ge(setup_gate, 2)
            tt(gate_size[:], g_row, gate_sign[:], ALU.mult).then_inc(setup_gate, 1)
            dve.wait_ge(setup_gate, 3)
            stt(gate_rows[:], gate_size[:], 0.25, gate_sign[:], ALU.max, ALU.mult).then_inc(setup_v, 1)
            dve.wait_ge(setup_v, SETUP_V)

            def add_expert(b, n):
                e, t = divmod(n, NT)
                if t == 0:
                    dve.wait_ge(out1_mm.sem, out1_mm.at(b, (e + 1) * NT))
                dve.wait_ge(out1_add.sem, out1_add.at(b, 1 if e == 0 else n - NT + 2))
                stt(expert_sum[:, t, :], bank[OUT1_BANK[e]][:, t * P:(t + 1) * P], gates[1][:, t, e:e + 1],
                    expert_sum[:, t, :], ALU.mult, ALU.add).then_inc(out1_add.sem, 1)

            def finish(b):
                dve.wait_ge(out1_add.sem, out1_add.at(b, E * NT + 1))
                dve.wait_ge(x_sent.sem, x_sent.before(b))
                tt(expert_out[:], expert_sum[:], gate[:, bass.ds(b, 1), 3, :].to_broadcast([P, NT, P]), ALU.mult
                   ).then_inc(out1_gate.sem, 1)
                dve.wait_ge(out1_gate.sem, out1_gate.at(b, 1))
                tt(x_out[:], x_mid[:], expert_out[:], ALU.add).then_inc(x_final.sem, 1)

            def ln_half_stats(half, x):
                for t in range(2 * half, 2 * half + 2):
                    ins = v.bn_stats(stats[:, t, :], x[:, t, :])
                return ins

            def ln_aggregate(link):
                v.memset(newton[:], 0.0)
                for t in range(NT):
                    ins = v.bn_aggr(meanvar[:, t, :], stats[:, t, :])
                link(ins)

            def ln_stats(b, j, x, link):
                ln_half_stats(0, x)
                link(ln_half_stats(1, x))
                ln_aggregate(link)

            def ln_normalise(b, j, x, mark, link):
                link(ts(var_eps[:], meanvar[:, :, 1], EPS, None, ALU.add))
                link(ts(rstd[:].bitcast(I32), var_eps[:].bitcast(I32), -0.5, ROOT_GUESS, ALU.mult, ALU.add))
                for _ in range(3):
                    link(tt(newton[:], rstd[:], rstd[:], ALU.mult))
                    link(stt(newton2[:], newton[:], -0.5, var_eps[:], ALU.mult, ALU.mult))
                    link(stt(rstd[:], newton2[:], 1.5, rstd[:], ALU.add, ALU.mult))
                link(stt(shift[:], meanvar[:, :, 0], -1.0, rstd[:], ALU.mult, ALU.mult))
                for t in range(NT):
                    ins = ts(xn[:, t, :], x[:, t, :], rstd[:, t:t + 1], shift[:, t:t + 1], ALU.mult, ALU.add)
                ins.then_inc(of(ln_xn, j), 1)

            def add_mixed(b, k, source, to, done, link):
                g_row = gate[:, bass.ds(b, 1), k, :].to_broadcast([P, NT, P])
                link(tt(mixed[:], source, g_row, ALU.mult))
                tt(to[:], x[:], mixed[:], ALU.add).then_inc(done.sem, 1)

            def choose(b, layer, link):
                wide = [P, NT, E]
                dve.wait_ge(log_mm.sem, log_mm.at(b, layer + 1))
                order = w["order"][:].unsqueeze(1).to_broadcast(wide)
                link(cp(logits[:], bank[MISC][:, 0:NT * E].rearrange("p (t e) -> p t e", e=E)))
                for k, (pick, values) in enumerate(((pick1, logits), (pick2, r_b))):
                    link(v.reduce_max(top[:, k, :], values[:], AX_X))
                    if k == 1:
                        tt(gap[:], top[:, 1, :], top[:, 0, :], ALU.subtract).then_inc(gap_in.sem, 1)
                    link(tt(r_a[:], values[:], top[:, k, :].unsqueeze(2).to_broadcast(wide), ALU.is_equal))
                    link(tt(r_a[:], r_a[:], order, ALU.mult))
                    link(v.reduce_max(best[:, k, :], r_a[:], AX_X))
                    link(tt(pick[:], r_a[:], best[:, k, :].unsqueeze(2).to_broadcast(wide), ALU.is_equal))
                    if k == 0:
                        link(stt(r_b[:], pick[:], FAR, logits[:], ALU.mult, ALU.add))

            def weigh(b, layer, mark, link):
                wide = [P, NT, E]
                dve.wait_ge(gap_out.sem, gap_out.at(b, layer + 1))
                link(ts(gap_one[:], gap_exp[:], 1.0, None, ALU.add))
                link(v.reciprocal(share1[:], gap_one[:]))
                link(tt(share2[:], share1[:], gap_exp[:], ALU.mult))
                mark(tt(r_a[:], pick1[:], share1[:].unsqueeze(2).to_broadcast(wide), ALU.mult))
                link(tt(r_b[:], pick2[:], share2[:].unsqueeze(2).to_broadcast(wide), ALU.mult))
                if layer == 0:
                    link(tt(gates[0][:], r_a[:], r_b[:], ALU.add))
                    cp(gates_wide[:].rearrange("p t e f -> p (t e) f"),
                       gates[0][:].rearrange("p t e -> p (t e)").unsqueeze(2).to_broadcast([P, NT * E, F0])
                       ).then_inc(gates_ok.sem, 1)
                else:
                    tt(gates[1][:], r_a[:], r_b[:], ALU.add).then_inc(gates_ok.sem, 1)

            def norm_step(b, j, k, x, steps):
                if k > 0:
                    dve.wait_ge(steps.sem, steps.at(b, k))
                elif j == 0:
                    dve.wait_ge(x_loaded.sem, x_loaded.at(b, 16))
                else:
                    dve.wait_ge(mix_add.sem, mix_add.at(b, 1))
                if k == 0:
                    for t in range(NT):
                        ins = v.bn_stats(stats[:, t, :], x[:, t, :])
                elif k == 1:
                    v.memset(newton[:], 0.0)
                    for t in range(NT):
                        ins = v.bn_aggr(meanvar[:, t, :], stats[:, t, :])
                elif k == 2:
                    ins = ts(var_eps[:], meanvar[:, :, 1], EPS, None, ALU.add)
                elif k == 3:
                    ins = ts(rstd[:].bitcast(I32), var_eps[:].bitcast(I32), -0.5, ROOT_GUESS, ALU.mult, ALU.add)
                elif k in (4, 7, 10):
                    ins = tt(newton[:], rstd[:], rstd[:], ALU.mult)
                elif k in (5, 8, 11):
                    ins = stt(newton2[:], newton[:], -0.5, var_eps[:], ALU.mult, ALU.mult)
                elif k in (6, 9, 12):
                    ins = stt(rstd[:], newton2[:], 1.5, rstd[:], ALU.add, ALU.mult)
                elif k == 13:
                    ins = stt(shift[:], meanvar[:, :, 0], -1.0, rstd[:], ALU.mult, ALU.mult)
                else:
                    for t in range(NT):
                        ins = ts(xn[:, t, :], x[:, t, :], rstd[:, t:t + 1], shift[:, t:t + 1], ALU.mult, ALU.add)
                ins.then_inc(steps.sem if k < NORM_STEPS - 1 else of(ln_xn, j), 1)

            def take_x(b):
                cp(x[:], x_in[:]).then_inc(x_taken.sem, 1)
                dve.wait_ge(x_taken.sem, x_taken.at(b, 1))

            def mixer_end(b, k, tail):
                mark, link, check = tail
                if k == 0:
                    dve.wait_ge(acc_ok.sem, acc_ok.at(b, NS - 1))
                    for c in range(DH):
                        link(stt(y_skip[:, c, :], xc[:, c, :], w["d_skip"][:, c:c + 1], state_sum[:, c, :],
                                 ALU.mult, ALU.add))
                        tt(z[:, c, :], y_skip[:, c, :], res_gate[:, c, :], ALU.mult).then_inc(z_ok.sem, 1)
                else:
                    dve.wait_ge(mix_mm.sem, mix_mm.at(b, 1))
                    link(tt(mixer_out[:], bank[OUT_BANK][:].rearrange("p (t d) -> p t d", d=P),
                            w["out_b"][:].unsqueeze(1).to_broadcast([P, NT, P]), ALU.add))
                    add_mixed(b, 2, mixer_out[:], x_mid, mix_add, link)
                    check()
                    dve.wait_ge(mix_add.sem, mix_add.at(b, 1))

            def expert_head(b, k, head):
                mark, link, check = head
                if k == 0:
                    choose(b, 1, link)
                elif k == 1:
                    weigh(b, 1, mark, link)
                    check()
                else:
                    dve.wait_ge(b2_mm.sem, b2_mm.at(b, 1))
                    cp(expert_sum[:].rearrange("p t d -> p (t d)"), bank[MISC][:]).then_inc(out1_add.sem, 1)

            def iteration(b, behind, ahead):
                mark, link, check = linker(dve, chain, b)
                if behind:
                    tail = linker(dve, chain_tail, b - 1)
                    head = linker(dve, chain_head, b - 1)
                def early(e):
                    if behind:
                        for t in range(NT):
                            add_expert(b - 1, e * NT + t)

                def row_maximum(n):
                    i = n // HG % NT
                    dve.wait_ge(s_mm.sem, s_mm.at(b, n + 1))
                    if n >= 4:
                        dve.wait_ge(s_exp.sem, s_exp.at(b, n - 3))
                    v.reduce_max(row_neg[:, n % 4:n % 4 + 1], bank[n % 4][:, 0:(i + 1) * P], AX_X, negate=True
                                 ).then_inc(s_max.sem, 1)

                def take_transposed(n):
                    dve.wait_ge(p_T.sem, p_T.at(b, n + 1))
                    if n >= UNITS // 2 and n % 8 == 0:
                        dve.wait_ge(y_mm.sem, y_mm.at(b, n // 8 - 1))
                    to, source = transposed(n)
                    cp(to, source).then_inc(p_out_v.sem, 1)

                def widen(half):
                    g, first = half // 2, half % 2 * 2
                    dve.wait_ge(s_exp.sem, s_exp.at(b, 8 * half + 8))
                    link(v.reciprocal(row_inv[:], row_sum[:, g, first:first + 2, :]))
                    cp(inv_wide[:].rearrange("p t h l -> p (t h) l"),
                       row_inv[:].rearrange("p t h -> p (t h)").unsqueeze(2).to_broadcast([P, 2 * HG, L])
                       ).then_inc(inv_w.sem, 1)

                def normalise(half):
                    g, first = half // 2, half % 2 * 2
                    dve.wait_ge(inv_out.sem, inv_out.at(b, half + 1))
                    tt(y_T[:, g, first * P:(first + 2) * P], bank[OUT_BANK][:, 0:2 * P], inv_T[:], ALU.mult
                       ).then_inc(y_out.sem, 1)

                for n in range(UNITS + LAG):
                    if n < UNITS:
                        row_maximum(n)
                    if n in (9, 17, 25, 33):
                        widen(n // 8 - 1)
                    if n in (15, 23, 31):
                        normalise(n // 8 - 1)
                    if n - LAG in BY_DVE:
                        take_transposed(n - LAG)
                    if behind:
                        if n in (1, 6):
                            mixer_end(b - 1, (1, 6).index(n), tail)
                        if n == 6:
                            take_x(b)
                        if 7 <= n < 7 + NORM_UNITS:
                            for k in range(2 * (n - 7), min(2 * (n - 6), NORM_STEPS)):
                                norm_step(b - 1, 3, k, x_mid, chain_norm)
                        if n in DVE_HEAD:
                            expert_head(b - 1, DVE_HEAD.index(n), head)
                if not behind:
                    take_x(b)
                normalise(3)
                for half in range(2):
                    dve.wait_ge(attn_mm.sem, attn_mm.at(b, half + 1))
                    tiles = slice(2 * half, 2 * half + 2)
                    g_row = gate[:, bass.ds(b, 1), 0, :].to_broadcast([P, 2, P])
                    source = bank[ATTN_BANK[half]][:, 2 * half * P:(2 * half + 2) * P].rearrange("p (t d) -> p t d", d=P)
                    link(tt(mixed[:, tiles, :], source, g_row, ALU.mult))
                    tt(x[:, tiles, :], x[:, tiles, :], mixed[:, tiles, :], ALU.add).then_inc(attn_add.sem, 1)
                    dve.wait_ge(attn_add.sem, attn_add.at(b, half + 1))
                    ins = ln_half_stats(half, x)
                link(ins)
                ln_aggregate(link)

                ln_normalise(b, 1, x, mark, link)
                choose(b, 0, link)
                weigh(b, 0, mark, link)
                for c in range(C0):
                    dve.wait_ge(hid0_act.sem, hid0_act.at(b, c + 1))
                    dve.wait_ge(gT_mm.sem, gT_mm.at(b, c + 1))
                    tt(gated[:, c, :], hid0[:, c, :], bank[GATE_BANK[c % 2]][:], ALU.mult).then_inc(hid0_gate.sem, 1)
                dve.wait_ge(out0_mm.sem, out0_mm.at(b, 1))
                add_mixed(b, 1, bank[OUT_BANK][:].rearrange("p (t d) -> p t d", d=P), x, out0_add, link)
                dve.wait_ge(out0_add.sem, out0_add.at(b, 1))

                ln_stats(b, 2, x, link)
                ln_normalise(b, 2, x, mark, link)
                early(0)
                for k in range(KC):
                    for c in range(DH):
                        if k == 0:
                            dve.wait_ge(in_out.sem, in_out.at(b, c + 1))
                            ins = ts(conv[0][:, c, :], xi[:, c, 0:T], w["conv_w"][:, c, 0:1], w["conv_b"][:, c:c + 1],
                                     ALU.mult, ALU.add)
                        else:
                            dve.wait_ge(taps.sem, taps.at(b, DH * (k - 1) + c + 1))
                            ins = stt(conv[k % 2][:, c, :], xi[:, c, k:k + T], w["conv_w"][:, c, k:k + 1],
                                      conv[(k - 1) % 2][:, c, :], ALU.mult, ALU.add)
                        ins.then_inc(taps.sem if k < KC - 1 else conv_ok.sem, 1)
                early(1)
                dve.wait_ge(pr_out.sem, pr_out.at(b, 1))
                link(cp(split[:], proj[0:3 * BC, :]))
                for lo, hi in ((L, 2 * L), (2 * L, 3 * L)):
                    link(tt(part[lo:hi, :], proj[lo:hi, :], split[lo:hi, :], ALU.subtract))
                    link(cp(split[lo:hi, :], part[lo:hi, :]))
                lo = 2 * L
                link(tt(part2[lo:lo + L, :], part[lo:lo + L, :], split[lo:lo + L, :], ALU.subtract))
                cp(split[lo:lo + L, :], part2[lo:lo + L, :]).then_inc(split_ok.sem, 1)
                for c in range(DH):
                    dve.wait_ge(chain_a.sem, chain_a.at(b, c + 1))
                    ts(dt_in[:, c, :], bank[HID0_BANK[c]][:], w["dt_b"][:, c:c + 1], None, ALU.add).then_inc(dt_z.sem, 1)
                for c in range(DH):
                    dve.wait_ge(dt_z.sem, dt_z.at(b, c + 1))
                    dve.wait_ge(dt_l.sem, dt_l.at(b, c + 1))
                    stt(delta[:, c, :], dt_in[:, c, :], 0.0, dt_log[:, c, :], ALU.max, ALU.add).then_inc(delta_ok.sem, 1)
                for c in range(DH):
                    dve.wait_ge(delta_ok.sem, delta_ok.at(b, c + 1))
                    tt(u[:, c, :], delta[:, c, :], xc[:, c, :], ALU.mult).then_inc(u_ok.sem, 1)
                dve.wait_ge(u_ok.sem, u_ok.at(b, DH))

                def inject_state(n):
                    if by_pool(n):
                        return
                    dve.wait_ge(b_mm.sem, b_mm.at(b, n + 1))
                    tt(inject[:, n % 2, :, :], u[:], bank[BC_BANK[0]][:].unsqueeze(1).to_broadcast([P, DH, T]), ALU.mult
                       ).then_inc(inj_v.sem, 1)

                def norm_beside_scan(k):
                    if ahead and 9 <= k < 9 + NORM_STEPS:
                        norm_step(b + 1, 0, k - 9, x_in, chain_pre)

                inject_state(0)
                for n in range(NS):
                    if n + 1 < NS:
                        inject_state(n + 1)
                    for c in range(DH):
                        norm_beside_scan(3 * n + c)
                        dve.wait_ge(dec_ok.sem, dec_ok.at(b, DH * n + c + 1))
                        if c == 0:
                            injected(dve, b, n)
                        v.tensor_tensor_scan(state[:, n % 2, c, :], decay[:, n % 4, c, :], inject[:, n % 2, c, :], 0.0,
                                             ALU.mult, ALU.add).then_inc(st_ok.sem, 1)
                    if n in (1, 5, 8, 10, 14):
                        early(EARLY_E + (1, 5, 8, 10, 14).index(n))
                    norm_beside_scan(3 * n + 2)
                    dve.wait_ge(c_mm.sem, c_mm.at(b, n + 1))
                    dve.wait_ge(st_ok.sem, st_ok.at(b, DH * (n + 1)))
                    if n >= 2:
                        dve.wait_ge(acc_ok.sem, acc_ok.at(b, max(1, n - 2)))
                    tt(read[:, n % 2, :, :], state[:, n % 2, :, :],
                       bank[BC_BANK[1]][:].unsqueeze(1).to_broadcast([P, DH, T]), ALU.mult).then_inc(rd_ok.sem, 1)
                if behind:
                    for n in range(E * NT - 4, E * NT):
                        add_expert(b - 1, n)
                    finish(b - 1)
                check()

            for k in range(NORM_STEPS):
                norm_step(0, 0, k, x_in, chain_pre)
            dve.wait_ge(setup_a, SETUP_A)
            iteration(0, False, True)
            with dve.Fori(1, B - 1) as b:
                iteration(b, True, True)
            iteration(B - 1, True, False)
            tail = linker(dve, chain_tail, B - 1)
            for k in range(2):
                mixer_end(B - 1, k, tail)
            head = linker(dve, chain_head, B - 1)
            for k in range(NORM_STEPS):
                norm_step(B - 1, 3, k, x_mid, chain_norm)
            for k in range(3):
                expert_head(B - 1, k, head)
            for n in range(E * NT):
                add_expert(B - 1, n)
            finish(B - 1)


CHAIN = {"tail": 4, "main": 59, "head": 17, "act main": 4}
NORM_STEPS = 15
NORM_UNITS = 8
ALL_BY_ACT = 12
LAG = 3
PE_HEAD, ACT_HEAD, DVE_HEAD = (16, 18, 25, 28), (17, 22, 26), (20, 23, 30)
SCAN_HIDDEN = {1: (14, 17), 2: (17, 20), 4: (20, 22), 5: (22, 24), 6: (24, 26), 7: (26, 28), 9: (28, 30), 10: (30, 32)}
SCAN_OUTPUT = {3: (12, 16), 4: (16, 17), 5: (17, 18), 6: (18, 20), 7: (20, 21), 8: (21, 24), 11: (24, 26),
               12: (26, 28), 13: (28, 30), 14: (30, 32)}
LATE = ("w1", "w2")
SETUP_V = 8
SETUP_A = 4 + B


def _laid_out(a):
    c = lambda v: np.ascontiguousarray(v)
    g = {k: np.asarray(v) for k, v in a.items()}
    chunks = lambda v, n: c(v.reshape(n, P, -1).transpose(1, 0, 2))
    o = {"x": g["L0_attn_x"]}
    o["wqT"] = c(g["L0_attn_wq"].reshape(P, H, P).transpose(2, 1, 0))
    o["wk_upT"] = c(g["L0_attn_wk_up"].T)
    o["wv_upT"] = c(g["L0_attn_wv_up"].T)
    o["wk4"] = c(np.repeat(g["L0_attn_wk_down"].reshape(P, G, 1, L), HG, axis=2).reshape(P, G, HG * L))
    o["wv_down"] = g["L0_attn_wv_down"]
    o["wo"] = chunks(g["L0_attn_wo"], H)
    o["wg0"] = c(g["L0_ffn_w_gate"].T)
    o["wfcT"] = c(g["L0_ffn_w_fc"].reshape(E * F0, P).T)
    o["wprojT"] = chunks(g["L0_ffn_w_proj"].transpose(0, 2, 1).reshape(E * F0, P), C0)
    o["cT"] = c(np.stack([g["L0_c"].T, g["L1_c"].T], axis=1))
    o["wmod"] = c(np.stack([g["L0_wmod"], g["L1_wmod"]], axis=1))
    o["in_w"] = g["L1_attn_in_proj_w"]
    o["in_b"] = c(g["L1_attn_in_proj_b"].reshape(2 * DH, P).T)
    o["conv_w"] = c(g["L1_attn_conv_w"].reshape(KC, DH, P).transpose(2, 1, 0))
    o["conv_b"] = c(g["L1_attn_conv_b"].reshape(DH, P).T)
    order = np.concatenate([np.arange(NS, 3 * NS)] * 3 + [np.arange(NS)])
    o["x_proj_w"] = chunks(g["L1_attn_x_proj_w"][:, order], DH)
    o["x_proj_b"] = c(g["L1_attn_x_proj_b"][order].reshape(PR, 1))
    dt_w = np.zeros((PR, DI), np.float32)
    dt_w[3 * BC:] = g["L1_attn_dt_proj_w"]
    o["dt_w"] = dt_w
    o["dt_b"] = c(g["L1_attn_dt_proj_b"].reshape(DH, P).T)
    o["a_log"] = c(g["L1_attn_A_log"].reshape(DH, P, NS).transpose(1, 0, 2))
    o["d_skip"] = c(g["L1_attn_D_skip"].reshape(DH, P).T)
    o["out_w"] = chunks(g["L1_attn_out_proj_w"], DH)
    o["out_b"] = c(np.broadcast_to(g["L1_attn_out_proj_b"], (P, P)))
    o["wg1"] = g["L1_ffn_gate_w"]
    o["w1"] = c(g["L1_ffn_w1"].transpose(1, 0, 2))
    o["b1"] = c(g["L1_ffn_b1"].reshape(E * C1, P).T)
    o["w2"] = chunks(g["L1_ffn_w2"].reshape(E * F1, P), E * C1)
    o["b2"] = g["L1_ffn_b2"]
    o["ident"] = np.eye(P, dtype=np.float32)
    o["mask"] = np.triu(np.full((P, P), FAR, np.float32), 1)
    o["stack"] = np.tile(np.eye(BC, dtype=np.float32), (3, 1))
    o["order"] = c(np.broadcast_to(np.arange(E, 0, -1, dtype=np.float32), (P, E)))
    return o


def kernel(**inputs):
    import concourse.bacc as bacc
    from concourse.bass_utils import run_bass_kernel_spmd

    nc = bacc.Bacc("TRN2", target_bir_lowering=False, num_devices=1)
    arrays, io = {}, {}
    for name, a in _laid_out(inputs).items():
        a = np.ascontiguousarray(a)
        arrays[f"in_{name}_dram"] = a
        io[name] = nc.dram_tensor(f"in_{name}_dram", a.shape, mybir.dt.from_np(a.dtype), kind="ExternalInput").ap()
    out = nc.dram_tensor("out_0_dram", (B, T, P), F32, kind="ExternalOutput").ap()
    nc.disable_value_cache = True
    build(nc, io, out)
    r = run_bass_kernel_spmd(nc, [arrays], core_ids=[0])
    return r.results[0]["out_0_dram"]
```
